# Optimizing a Trainium2 kernel written in Bass

```python
import numpy as np
import jax
import jax.numpy as jnp

def _softmax(x, axis=-1):
    return jax.nn.softmax(x, axis=axis)

def _gelu(x):
    return jax.nn.gelu(x, approximate=True)

def _silu(x):
    return jax.nn.silu(x)

def _sigmoid(x):
    return jax.nn.sigmoid(x)

def _layernorm(x, axis=-1, eps=1e-05):
    m = jnp.mean(x, axis=axis, keepdims=True)
    v = jnp.var(x, axis=axis, keepdims=True)
    return (x - m) / jnp.sqrt(v + eps)

def _scatter_add(tgt, idx, src, axis=0):
    return tgt.at[idx].add(src)

def _segment_sum(src, seg, n):
    return jax.ops.segment_sum(src, seg, n)
kernel_name = 'mk_audio_tower_d1_tok_audfeat256_r4_1d9ae4'

def setup_inputs(seed: int=0):
    np.random.seed(seed)
    _w = jnp.asarray

    def _rec_inputs():
        import jax
        import jax.numpy as jnp
        _rk = jax.random.key(seed)
        x = -7.10856e-05 + 0.999911 * jax.random.normal(jax.random.fold_in(_rk, 1), (64, 64, 375), jnp.float32)
        return x
    x = _rec_inputs()

    def _L0_tok_setup():
        import jax, jax.numpy as jnp
        import numpy as np
        KERNEL_SIZE = 8
        key = jax.random.key(seed)
        k1, k2 = jax.random.split(key)
        B, F, T = (16, 64, 4096)
        x = jax.random.normal(k1, (B, F, T), dtype=jnp.float32)
        w = jax.random.normal(k2, (1, F), dtype=jnp.float32) * 0.05
        b = jnp.zeros((1,), dtype=jnp.float32)
        return {'x': x, 'w': w, 'b': b}
    _L0_tok_all = _L0_tok_setup()
    _L0_tok_in = {k: v for k, v in _L0_tok_all.items() if k in ('w', 'b')}
    del _L0_tok_all

    def _L0_attn_setup():
        import jax, jax.numpy as jnp
        import numpy as np
        from math import sqrt
        DIM = 64
        key = jax.random.key(seed)
        k1, k2, k3, k4 = jax.random.split(key, 4)
        B, T, D, H, R = (2, 1024, DIM, 8, 32)

        def xavier(k, shape, fan_in, fan_out):
            a = sqrt(6.0 / (fan_in + fan_out))
            return jax.random.uniform(k, shape, jnp.float32, -a, a)
        x = jax.random.normal(k1, (B, T, D), jnp.float32)
        Q = xavier(k2, (H, R, D), D, R)
        K = xavier(k3, (H, R, D), D, R)
        VO = xavier(k4, (H, D, D), D, D)
        return {'x': x, 'Q': Q, 'K': K, 'VO': VO}
    _L0_attn_all = _L0_attn_setup()
    _L0_attn_in = {k: v for k, v in _L0_attn_all.items() if k in ('Q', 'K', 'VO')}
    del _L0_attn_all

    def _L0_ffn_setup():
        import jax, jax.numpy as jnp
        import numpy as np
        C = 64
        HID = 256
        E = 8
        TEMP = 1.0
        key = jax.random.key(seed)
        ks = jax.random.split(key, 7)
        x = jax.random.normal(ks[0], (8, 4096, C), dtype=jnp.float32)
        W1 = jax.random.normal(ks[1], (C, HID), dtype=jnp.float32) * 0.02
        b1 = jnp.zeros((HID,), dtype=jnp.float32)
        Wg = jax.random.normal(ks[2], (HID, E), dtype=jnp.float32) * 0.02
        bg = jnp.zeros((E,), dtype=jnp.float32)
        Wd = jax.random.normal(ks[3], (E, HID, C), dtype=jnp.float32) * 0.02
        bd = jnp.zeros((E, C), dtype=jnp.float32)
        return {'x': x, 'W1': W1, 'b1': b1, 'Wg': Wg, 'bg': bg, 'Wd': Wd, 'bd': bd}
    _L0_ffn_all = _L0_ffn_setup()
    _L0_ffn_in = {k: v for k, v in _L0_ffn_all.items() if k in ('W1', 'b1', 'Wg', 'bg', 'Wd', 'bd')}
    del _L0_ffn_all
    return {'x': x, 'L0_tok_w': _L0_tok_in['w'], 'L0_tok_b': _L0_tok_in['b'], 'L0_attn_Q': _L0_attn_in['Q'], 'L0_attn_K': _L0_attn_in['K'], 'L0_attn_VO': _L0_attn_in['VO'], 'L0_ffn_W1': _L0_ffn_in['W1'], 'L0_ffn_b1': _L0_ffn_in['b1'], 'L0_ffn_Wg': _L0_ffn_in['Wg'], 'L0_ffn_bg': _L0_ffn_in['bg'], 'L0_ffn_Wd': _L0_ffn_in['Wd'], 'L0_ffn_bd': _L0_ffn_in['bd']}

def reference(x, L0_tok_w, L0_tok_b, L0_attn_Q, L0_attn_K, L0_attn_VO, L0_ffn_W1, L0_ffn_b1, L0_ffn_Wg, L0_ffn_bg, L0_ffn_Wd, L0_ffn_bd):
    import jax
    import jax.numpy as jnp

    def _L0_tok_ref(x, w, b):
        import jax, jax.numpy as jnp
        import numpy as np
        KERNEL_SIZE = 8
        k = KERNEL_SIZE
        B, F, T = x.shape
        pad = -T % k
        if pad:
            x = jnp.pad(x, ((0, 0), (0, 0), (0, pad)))
            T += pad
        nw = T // k
        xp = x.reshape(B, F, nw, k).transpose(0, 2, 3, 1)
        scores = jnp.einsum('bwkf,of->bwko', xp, w) + b
        weights = jax.nn.softmax(scores, axis=2)
        pooled = jnp.sum(xp * weights, axis=2)
        return pooled

    def _L0_attn_ref(x, Q, K, VO):
        import jax, jax.numpy as jnp
        import numpy as np
        from math import sqrt
        DIM = 64
        d = x.shape[-1]
        q = jnp.einsum('btd,hrd->bhtr', x, Q)
        k = jnp.einsum('bud,hrd->bhur', x, K)
        scores = jnp.einsum('bhtr,bhur->bhtu', q, k) / sqrt(d)
        attn = jax.nn.softmax(scores, axis=-1)
        ctx = jnp.einsum('bhtu,bud->bhtd', attn, x)
        out = jnp.einsum('bhtd,hde->bte', ctx, VO)
        return out

    def _L0_ffn_ref(x, W1, b1, Wg, bg, Wd, bd):
        import jax, jax.numpy as jnp
        import numpy as np
        C = 64
        HID = 256
        E = 8
        TEMP = 1.0
        orig_shape = x.shape
        xf = x.reshape(-1, orig_shape[-1])
        H = jax.nn.gelu(xf @ W1 + b1, approximate=False)
        probs = jax.nn.softmax((H @ Wg + bg) / TEMP, axis=-1)
        assign = jnp.argmax(probs, axis=-1)
        out = jnp.zeros_like(xf)
        for e in range(Wd.shape[0]):
            y = H @ Wd[e] + bd[e]
            sel = (assign == e)[:, None]
            out = out + jnp.where(sel, probs[:, e:e + 1] * y, 0.0)
        return out.reshape(orig_shape)
    h = _L0_tok_ref(x, L0_tok_w, L0_tok_b)
    h = h + _L0_attn_ref(_layernorm(h, axis=-1), L0_attn_Q, L0_attn_K, L0_attn_VO)
    h = h + _L0_ffn_ref(_layernorm(h, axis=-1), L0_ffn_W1, L0_ffn_b1, L0_ffn_Wg, L0_ffn_bg, L0_ffn_Wd, L0_ffn_bd)
    return h

_drawn_inputs = setup_inputs


def setup_inputs(seed=0):
    import zlib

    import numpy as np

    out = dict(_drawn_inputs(seed))
    spreads = {'L0_ffn_b1': (0.0, 0.8), 'L0_ffn_bg': (0.0, 0.365), 'L0_ffn_bd': (0.0, 0.519)}
    factors = {'L0_ffn_W1': 8.0, 'L0_ffn_Wg': 8.0, 'L0_ffn_Wd': 8.0}
    for name, (base, spread) in spreads.items():
        noise = np.random.default_rng([zlib.crc32(name.encode()), seed]).standard_normal(out[name].shape)
        drawn = base * np.exp(spread * noise) if base else spread * noise
        out[name] = jnp.asarray(drawn.astype(out[name].dtype))
    for name, factor in factors.items():
        out[name] = (out[name] * factor).astype(out[name].dtype)
    return out
```

```python
from contextlib import ExitStack

import concourse.bass as bass
from concourse import mybir

F32 = mybir.dt.float32
BF16 = mybir.dt.bfloat16
ALU = mybir.AluOpType
ACT = mybir.ActivationFunctionType
AX = mybir.AxisListType


def audio_tower_kernel(nc, x, tok_w, tok_b, Q, K, VO, W1, b1, Wg, bg, Wd, bd, out):
    B, F, T_RAW = x.shape
    WIN = 8
    NW = -(-T_RAW // WIN)
    T = NW * WIN
    H, R, _ = Q.shape
    HID = W1.shape[1]
    E = Wg.shape[1]
    NPAIR = B // 2
    P = 128
    TP = 64
    HALF = NPAIR // 2
    HC = H // 2
    LNC = 8
    NLN = NPAIR // LNC
    LNW = LNC * NW
    NSTEP = NPAIR // 2
    G4 = 4 * NW
    LOOP_END = NSTEP - 4
    NF = 8
    FT = 8 * NW
    HCH = HID // P
    STARTS = [0, P, FT - P]
    SKIP = 2 * P - (FT - P)
    EC = E * F
    EPS = 1e-5

    with ExitStack() as ctx:
        def sb(name, shape, dt=F32):
            return ctx.enter_context(nc.sbuf_tensor(name, shape, dt))

        def ps(name, shape):
            return ctx.enter_context(nc.psum_tensor(name, shape, F32))

        def sem(name):
            return ctx.enter_context(nc.semaphore(name))

        x_sb = sb("x_sb", [P, NPAIR, T])
        wcol = sb("wcol", [P, 1])
        eps = sb("eps", [P, 1])
        tokb = sb("tokb", [P, 1])
        wscore = sb("wscore", [P, HALF * (96 + 2)])
        sel = sb("sel", [96, HALF, P], BF16)
        ident = sb("ident", [P, P])
        mean64 = sb("mean64", [P, P])
        ones3 = sb("ones3", [96, P], BF16)
        wmax = sb("wmax", [96, NW])
        wmaxb = sb("wmaxb", [96, NW])
        wexp = sb("wexp", [96, T])
        wsum = sb("wsum", [96, NW])
        wrec = sb("wrec", [96, NW])
        wprob = sb("wprob", [96, T])
        wrest = sb("wrest", [96, T])
        wmid = sb("wmid", [96, T], BF16)
        wpieces = sb("wpieces", [96, 2, T], BF16)
        prod = sb("prod", [P, 2, T])
        hT = sb("hT", [P, NPAIR, NW])
        xnT = sb("xnT", [P, NPAIR, NW])
        cen = sb("cen", [P, NLN, LNW])
        sq = sb("sq", [P, NLN, LNW])
        lnv = sb("lnv", [P, NLN, LNW])
        rstd = sb("rstd", [P, NLN, LNW])
        q_sb = sb("q_sb", [R, H, F])
        k_sb = sb("k_sb", [R, H, F])
        MM = sb("MM", [F, HC, P])
        VOz = sb("VOz", [P, 2, 4, P])
        XT = [sb(f"XT{s}", [P, 4, P]) for s in range(2)]
        XB = [sb(f"XB{s}", [P, 4, P]) for s in range(2)]
        G = [sb(f"G{s}", [P, HC, G4]) for s in range(2)]
        rmax = sb("rmax", [P, 16])
        D = sb("D", [P, 16, NW])
        Ex = sb("Ex", [P, 16, NW])
        rsum = sb("rsum", [P, 16])
        rrec = [sb(f"rrec{s}", [P, 16]) for s in range(2)]
        Pn = [sb(f"Pn{s}", [P, 16, TP]) for s in range(2)]
        PT = sb("PT", [P, 4, G4])
        C = sb("C", [P, 4, 4, NW])
        w1_sb = sb("w1_sb", [F, HID])
        b1_sb = sb("b1_sb", [P, HCH])
        wg_sb = sb("wg_sb", [P, HCH, E])
        bg_sb = sb("bg_sb", [P, E])
        wd_sb = sb("wd_sb", [P, HCH, E, F])
        bdrow = sb("bdrow", [96, EC])
        bdrest = sb("bdrest", [96, EC])
        bdmid = sb("bdmid", [96, EC], BF16)
        bd3 = sb("bd3", [96, EC], BF16)
        rank = sb("rank", [P, E])
        xq = [sb(f"xq{s}", [P, FT]) for s in range(2)]
        Hs = [sb(f"Hs{s}", [P, HCH, FT]) for s in range(2)]
        lg = sb("lg", [P, 3, E])
        lmax = sb("lmax", [P, 3])
        ld = sb("ld", [P, 3, E])
        le = sb("le", [P, 3, E])
        lsum = sb("lsum", [P, 3])
        lrec = sb("lrec", [P, 3])
        lscore = sb("lscore", [P, 3, E])
        lbest = sb("lbest", [P, 3])
        lmask = sb("lmask", [P, 3, E])
        gate = sb("gate", [P, 3, E])
        z = sb("z", [P, 2, E, F])
        ysel = sb("ysel", [P, 3, F])
        osb = [sb(f"osb{s}", [P, 3, F]) for s in range(2)]

        bank = ps("bank", [P, 8, 512])

        psScore = [bank[0:96, i, 0:T] for i in (0, 1)]
        psW = [bank[:, i, 0:T] for i in (2, 3)]
        psMM = bank[0:F, 4, :]
        psLN = [bank[:, i, 0:LNW] for i in (4, 5, 6, 7)]
        psG = bank[:, 0:2, :]
        psO = bank[:, 0, 384:384 + 2 * NW]
        psS = bank[:, 2:4, :]
        psT = bank[:, 4:6, :]
        psC = bank[:, 6:8, :]
        psH = [bank[:, i, 0:FT] for i in (0, 1)]
        psL = [bank[:, i, 0:3 * E] for i in (2, 3)]
        psR = [bank[:, i, 64:64 + 3 * F] for i in (2, 3)]
        psY = [bank[:, i, :] for i in (4, 5, 6)]

        NX = 8
        s_x = [sem(f"s_x{i}") for i in range(NX)]
        s_wload = sem("s_wload")
        s_aload = sem("s_aload")
        s_fload = sem("s_fload")
        s_bdload = sem("s_bdload")
        ALOADS = 16 * (2 + 8)
        s_zero = sem("s_zero")
        s_vz = sem("s_vz")
        s_pz = sem("s_pz")
        s_sel = sem("s_sel")
        s_idt = sem("s_idt")
        s_wsc = sem("s_wsc")
        s_rank = sem("s_rank")
        s_score = sem("s_score")
        s_wmax, s_wmaxb, s_wsub, s_wexp, s_wsum, s_wrec, s_wprob = [
            sem(n) for n in ("s_wmax", "s_wmaxb", "s_wsub", "s_wexp", "s_wsum", "s_wrec", "s_wprob")]
        s_wpc = sem("s_wpc")
        s_wbc = sem("s_wbc")
        s_prod = sem("s_prod")
        s_pool = sem("s_pool")
        s_mm = sem("s_mm")
        s_mmc = sem("s_mmc")
        s_mean = sem("s_mean")
        s_cen = sem("s_cen")
        s_sq = sem("s_sq")
        s_var = sem("s_var")
        s_ln = sem("s_ln")
        s_rstd = sem("s_rstd")
        s_xn = sem("s_xn")
        s_xt = [sem(f"s_xt{i}") for i in range(2)]
        s_g = sem("s_g")
        s_gev = sem("s_gev")
        s_s = sem("s_s")
        s_xtr = sem("s_xtr")
        s_xb = sem("s_xb")
        s_max = sem("s_max")
        s_sub = sem("s_sub")
        s_exp = sem("s_exp")
        s_sum = sem("s_sum")
        s_rec = sem("s_rec")
        s_pn = sem("s_pn")
        s_t = sem("s_t")
        s_pt = sem("s_pt")
        s_c = sem("s_c")
        s_cev = sem("s_cev")
        s_o = sem("s_o")
        s_res = sem("s_res")
        s_bd = sem("s_bd")
        s_xq = [sem(f"s_xq{i}") for i in range(2)]
        s_h = sem("s_h")
        s_gelu = sem("s_gelu")
        s_lg = sem("s_lg")
        s_y = sem("s_y")
        s_lgb, s_lmax, s_lsub, s_gexp, s_lsum, s_lrec, s_lscore, s_lbest, s_lmask, s_gate = [
            sem(n) for n in ("s_lgb", "s_lmax", "s_lsub", "s_gexp", "s_lsum", "s_lrec", "s_lscore", "s_lbest",
                             "s_lmask", "s_gate")]
        s_z = sem("s_z")
        s_ys = sem("s_ys")
        s_fin = sem("s_fin")
        s_out = [sem(f"s_out{i}") for i in range(2)]

        def after(eng, s, v):
            if not isinstance(v, int) or v > 0:
                eng.wait_ge(s, v)

        def steps(eng, first, last, lo, hi, body):
            for k in range(first, lo):
                body(k, k % 2, k // 2)
            if hi > lo:
                assert (hi + 1 - lo) % 2 == 0
                with eng.Fori(0, (hi + 1 - lo) // 2) as i:
                    for s in range(lo, lo + 2):
                        body(i * 2 + s, s % 2, i + s // 2)
            for k in range(max(hi, lo - 1) + 1, last + 1):
                body(k, k % 2, k // 2)

        def runs(k, n=NSTEP):
            return not isinstance(k, int) or 0 <= k < n

        def at(k, n):
            return slice(k, k + n) if isinstance(k, int) else bass.ds(k, n)

        block = ctx.enter_context(nc.Block())

        @block.sync
        def _(sp):
            xv = x.rearrange("(p b) f t -> (b f) p t", b=2)
            per = NPAIR // NX
            for i in range(NX):
                sp.dma_start(x_sb[:, i * per:(i + 1) * per, 0:T_RAW], xv[:, i * per:(i + 1) * per, :]).then_inc(s_x[i], 16)

            def load_xt(k, s, _):
                after(sp, s_xtr, k - 1)
                dst = XT[s][:, :, :].rearrange("p (r b) c -> p r b c", b=2)
                for b2 in range(2):
                    for par in range(2):
                        sp.dma_start(dst[par * TP:par * TP + F, :, b2, par * TP:par * TP + NW],
                                     xnT[b2 * F:b2 * F + F, at(k * 2, 2), :]).then_inc(s_xt[s], 16)

            sp.wait_ge(s_zero, 1)
            sp.wait_ge(s_xn, 1)
            load_xt(0, 0, 0)
            load_xt(1, 1, 0)
            sp.wait_ge(s_xn, NLN)
            steps(sp, 2, NSTEP - 1, 2, NSTEP - 1, load_xt)

            def load_xq(k, s, _):
                after(sp, s_lg, k - 1)
                for half, src in enumerate((xnT, hT)):
                    dst = xq[s][half * F:half * F + F, :].rearrange("p (r b t) -> p r b t", b=2, t=NW)
                    for b2 in range(2):
                        sp.dma_start(dst[:, :, b2, :], src[b2 * F:b2 * F + F, at(k * 4, 4), :]).then_inc(s_xq[s], 16)

            sp.wait_ge(s_xn, 2 * NLN)
            steps(sp, 0, NF - 1, 2, NF - 1, load_xq)

        @block.gpsimd
        def _(pool):
            pool.memset(ident[:, :], 0.0).then_inc(s_pz, 1)
            pool.memset(sel[:, :, :], 0.0).then_inc(s_pz, 1)
            pool.wait_ge(s_pz, 2)
            pool.affine_select(out=ident[:, :], in_=ident[:, :], compare_op=ALU.not_equal, fill=1.0,
                               base=0, pattern=[[-1, P]], channel_multiplier=1).then_inc(s_idt, 1)
            for j in range(3):
                pool.wait_ge(s_idt if j == 0 else s_sel, max(j, 1))
                v = sel[32 * j:32 * j + 32, :, :].rearrange("q i (b f) -> q i b f", b=2)
                pool.affine_select(out=v, in_=v, compare_op=ALU.not_equal, fill=1.0, base=0,
                                   pattern=[[-2, HALF], [-1, 2], [0, F]], channel_multiplier=1).then_inc(s_sel, 1)
            pool.wait_ge(s_sel, 3)
            for s in range(2):
                pool.memset(Pn[s][:, :, :], 0.0).then_inc(s_pz, 1)
            pool.wait_ge(s_pz, 4)
            for e in range(E):
                pool.memset(rank[:, e:e + 1], float(E - e)).then_inc(s_rank, 1)

            def normalise(k, s, _):
                pool.wait_ge(s_rec, k + 1)
                after(pool, s_t, k - 1)
                pool.tensor_tensor(Pn[s][:, :, 0:NW], Ex[:, :, :],
                                   rrec[s][:, :].unsqueeze(2).to_broadcast([P, 16, NW]),
                                   ALU.mult).then_inc(s_pn, 1)

            steps(pool, 0, NSTEP - 1, 2, NSTEP - 1, normalise)

            def store(k, s, _):
                pool.wait_ge(s_fin, k + 1)
                o = out.rearrange("b t c -> (b t) c")[at(k * FT, FT), :]
                pool.dma_start(o[0:2 * P, :].rearrange("(j p) c -> p j c", p=P), osb[s][:, 0:2, :]).then_inc(s_out[s], 16)
                pool.dma_start(o[2 * P:FT, :], osb[s][SKIP:P, 2, :]).then_inc(s_out[s], 16)

            steps(pool, 0, NF - 1, 0, NF - 1, store)
            for s in range(2):
                pool.wait_ge(s_out[s], 32 * (NF // 2))

        @block.scalar
        def _(act):
            wv = tok_w.rearrange("o f -> f o")
            for b2 in range(2):
                act.dma_start(wcol[b2 * F:b2 * F + F, :], wv).then_inc(s_wload, 16)
            act.dma_start(tokb[:, :], tok_b.rearrange("(o a) -> o a", a=1).to_broadcast([P, 1])).then_inc(s_wload, 16)
            act.dma_start(q_sb[:, :, :], Q.rearrange("h r d -> r h d")).then_inc(s_aload, 16)
            act.dma_start(k_sb[:, :, :], K.rearrange("h r d -> r h d")).then_inc(s_aload, 16)
            act.wait_ge(s_zero, 1)
            vov = VO.rearrange("(cc c2 par) d e -> c2 d cc par e", c2=2, par=2)
            for c2 in range(2):
                for b2 in range(2):
                    dst = VOz[c2 * F:c2 * F + F, b2, :, b2 * F:b2 * F + F].rearrange("d (cc par) e -> d cc par e", par=2)
                    for cc in range(2):
                        act.dma_start(dst[:, cc], vov[c2, :, cc]).then_inc(s_aload, 16)
            act.dma_start(w1_sb[:, :], W1).then_inc(s_fload, 16)
            act.dma_start(b1_sb[:, :], b1.rearrange("(c p) -> p c", p=P), allow_slow_non_contiguous=True).then_inc(s_fload, 16)
            act.dma_start(wg_sb[:, :, :], Wg.rearrange("(c p) e -> p c e", p=P)).then_inc(s_fload, 16)
            act.dma_start(bg_sb[:, :], bg.rearrange("(o e) -> o e", o=1).to_broadcast([P, E])).then_inc(s_fload, 16)
            for c in range(HCH):
                act.dma_start(wd_sb[:, c, :, :], Wd[:, c * P:(c + 1) * P, :].rearrange("e p c -> p e c")).then_inc(s_fload, 16)
            for j in range(3):
                act.dma_start(bdrow[32 * j:32 * j + 1, :], bd.rearrange("(o e) c -> o (e c)", o=1)).then_inc(s_bdload, 16)

            for hf in range(2):
                act.wait_ge(s_wsub, hf + 1)
                nc.scalar.activation(wexp[:, :], wexp[:, :], ACT.Exp).then_inc(s_wexp, 1)

            def layernorm(n):
                for c in range(NLN):
                    act.wait_ge(s_cen, n * NLN + c + 1)
                    nc.scalar.activation(sq[:, c, :], cen[:, c, :], ACT.Square).then_inc(s_sq, 1)
                for c in range(NLN):
                    act.wait_ge(s_var, n * NLN + c + 1)
                    nc.scalar.activation(lnv[:, c, :], psLN[c], ACT.Ln, bias=eps[:, 0:1]).then_inc(s_ln, 1)
                    act.wait_ge(s_ln, n * NLN + c + 1)
                    nc.scalar.activation(rstd[:, c, :], lnv[:, c, :], ACT.Exp, scale=-0.5).then_inc(s_rstd, 1)

            act.wait_ge(s_mm, 1)
            nc.scalar.copy(MM[:, :, :].rearrange("d c e -> d (c e)"), psMM).then_inc(s_mmc, 1)
            layernorm(0)

            def evac_g(k, s):
                act.wait_ge(s_g, k + 1)
                after(act, s_s, k - 1)
                nc.scalar.copy(G[s][:, :, :].rearrange("p (a c) n -> p a (c n)", a=2), psG[:, :, 0:2 * G4]).then_inc(s_gev, 1)

            def exp(k):
                act.wait_ge(s_sub, k + 1)
                after(act, s_pn, k)
                nc.scalar.activation(Ex[:, :, :], D[:, :, :], ACT.Exp, scale=float(F) ** -0.5).then_inc(s_exp, 1)

            def evac_t(k):
                act.wait_ge(s_t, k + 1)
                after(act, s_c, k)
                nc.scalar.copy(PT[:, :, :].rearrange("p b (g t) -> p (b g) t", t=NW),
                               psT.rearrange("p k (g t) -> p (k g) t", t=TP)[:, :, 0:NW]).then_inc(s_pt, 1)

            def evac_c(k):
                act.wait_ge(s_c, k + 1)
                after(act, s_o, k)
                nc.scalar.copy(C[:, :, :, :].rearrange("p (k b) g t -> p k b (g t)", k=2),
                               psC[:, :, 0:2 * G4].rearrange("p k (b n) -> p k b n", b=2)).then_inc(s_cev, 1)

            def step(k, s, _):
                if runs(k - 1):
                    evac_c(k - 1)
                if runs(k + 2):
                    evac_g(k + 2, s)
                if runs(k):
                    evac_t(k)
                if runs(k + 1):
                    exp(k + 1)

            steps(act, -2, NSTEP, 1, LOOP_END, step)
            layernorm(1)

            def gelu(k, s):
                act.wait_ge(s_h, k + 1)
                after(act, s_y, 3 * (k - 1))
                for c in range(HCH):
                    nc.scalar.activation(Hs[s][:, c, :], psH[c], ACT.Gelu, bias=b1_sb[:, c:c + 1]).then_inc(s_gelu, 1)

            def gate_exp(k):
                act.wait_ge(s_lsub, k + 1)
                nc.scalar.activation(le[:, :, :], ld[:, :, :], ACT.Exp).then_inc(s_gexp, 1)

            act.wait_ge(s_fload, 16 * 6)
            gelu(0, 0)

            def fstep(k, s, _):
                if runs(k + 1, NF):
                    gelu(k + 1, 1 - s)
                gate_exp(k)

            steps(act, 0, NF - 1, 1, NF - 2, fstep)

        @block.vector
        def _(dve):
            def link(ins, s, n):
                ins.then_inc(s, 1)
                dve.wait_ge(s, n)

            def split3(src, rest, mid, pieces, s, n):
                link(nc.vector.tensor_copy(pieces, src), s, n + 1)
                link(nc.vector.tensor_tensor(rest, src, pieces, ALU.subtract), s, n + 2)
                link(nc.vector.tensor_copy(mid, rest), s, n + 3)
                link(nc.vector.tensor_copy(pieces[32:64], mid[32:64]), s, n + 4)
                link(nc.vector.tensor_tensor(pieces[64:96], rest[64:96], mid[64:96], ALU.subtract), s, n + 5)

            nc.vector.memset(wscore[:, :], 0.0).then_inc(s_wsc, 1)
            nc.vector.memset(x_sb[:, :, T_RAW:T], 0.0).then_inc(s_wsc, 1)
            nc.vector.memset(eps[:, :], EPS).then_inc(s_wsc, 1)
            dve.wait_ge(s_wsc, 3)
            dve.wait_ge(s_wload, 48)
            for b2 in range(2):
                dst = wscore[b2 * F:b2 * F + F, :].rearrange("p (i c) -> p i c", c=98)[:, :, b2:b2 + 65:32]
                nc.vector.tensor_copy(dst, wcol[b2 * F:b2 * F + F, :].unsqueeze(2).to_broadcast([F, HALF, 3])).then_inc(s_wsc, 1)
            for v in (XT[0][:, :, :], XT[1][:, :, :], VOz[:, :, :, :]):
                nc.vector.memset(v, 0.0).then_inc(s_vz, 1)
            nc.vector.memset(bdrow[:, :], 0.0).then_inc(s_vz, 1)
            nc.vector.memset(mean64[:, :], 0.0).then_inc(s_vz, 1)
            dve.wait_ge(s_vz, 5)
            for b2 in range(2):
                nc.vector.memset(mean64[b2 * F:b2 * F + F, b2 * F:b2 * F + F], 1.0 / F).then_inc(s_vz, 1)
            dve.wait_ge(s_vz, 7)
            nc.vector.memset(ones3[:, :], 1.0).then_inc(s_zero, 1)

            win = "p (w k) -> p w k"
            def pool_tile(j, s, _):
                dve.wait_ge(s_wbc, j + 1)
                link(nc.vector.tensor_tensor(prod[:, s, :], x_sb[:, at(j, 1), :].rearrange("p o t -> p (o t)"),
                                             psW[s], ALU.mult), s_prod, j + 1)
                nc.vector.tensor_reduce(hT[:, at(j, 1), :].rearrange("p o t -> p (o t)"),
                                        prod[:, s, :].rearrange(win, k=WIN), AX.X, ALU.add).then_inc(s_pool, 1)

            for hf in range(2):
                n = hf + 1
                dve.wait_ge(s_score, n)
                sc = psScore[hf].rearrange(win, k=WIN)
                link(nc.vector.tensor_reduce(wmax[:, :], sc, AX.X, ALU.max), s_wmax, n)
                link(nc.vector.tensor_scalar(wmaxb[:, :], wmax[:, :], tokb[0:96, 0:1], None, ALU.add), s_wmaxb, n)
                nc.vector.scalar_tensor_tensor(
                    out=wexp[:, :].rearrange(win, k=WIN), in0=sc, scalar=tokb[0:96, 0:1],
                    in1=wmaxb[:, :].unsqueeze(2).to_broadcast([96, NW, WIN]), op0=ALU.add,
                    op1=ALU.subtract).then_inc(s_wsub, 1)
                dve.wait_ge(s_wexp, n)
                ex = wexp[:, :].rearrange(win, k=WIN)
                link(nc.vector.tensor_reduce(wsum[:, :], ex, AX.X, ALU.add), s_wsum, n)
                link(nc.vector.reciprocal(wrec[:, :], wsum[:, :]), s_wrec, n)
                link(nc.vector.tensor_tensor(wprob[:, :].rearrange(win, k=WIN), ex,
                                             wrec[:, :].unsqueeze(2).to_broadcast([96, NW, WIN]), ALU.mult), s_wprob, n)
                split3(wprob[:, :], wrest[:, :], wmid[:, :], wpieces[:, hf, :], s_wpc, 5 * hf)
                steps(dve, hf * HALF, (hf + 1) * HALF - 1, hf * HALF, (hf + 1) * HALF - 1, pool_tile)

            def layernorm(n):
                for c in range(NLN):
                    dve.wait_ge(s_mean, n * NLN + c + 1)
                    nc.vector.tensor_tensor(cen[:, c, :], hT[:, c * LNC:(c + 1) * LNC, :].rearrange("p r t -> p (r t)"),
                                            psLN[c], ALU.subtract).then_inc(s_cen, 1)
                for c in range(NLN):
                    dve.wait_ge(s_rstd, n * NLN + c + 1)
                    nc.vector.tensor_tensor(xnT[:, c * LNC:(c + 1) * LNC, :].rearrange("p r t -> p (r t)"),
                                            cen[:, c, :], rstd[:, c, :], ALU.mult).then_inc(s_xn, 1)

            dve.wait_ge(s_pool, NPAIR)
            layernorm(0)

            sS = psS[:, :, 0:2 * G4].rearrange("p k (g u) -> p k g u", u=NW)

            def max_sub(k):
                dve.wait_ge(s_xtr, k + 1)
                link(nc.vector.tensor_reduce(rmax[:, :].rearrange("p (k g) -> p k g", k=2), sS, AX.X, ALU.max), s_max, k + 1)
                after(dve, s_exp, k)
                nc.vector.tensor_tensor(D[:, :, :].rearrange("p (k g) u -> p k g u", k=2), sS,
                                        rmax[:, :].rearrange("p (k g) -> p k g", k=2).unsqueeze(3).to_broadcast([P, 2, 8, NW]),
                                        ALU.subtract).then_inc(s_sub, 1)

            def evac_xb(k, s):
                after(dve, s_c, k - 1)
                nc.vector.tensor_copy(XB[s][:, 0:2, :], psS[:, :, 384:512]).then_inc(s_xb, 1)
                nc.vector.tensor_copy(XB[s][:, 2:4, :], psC[:, :, 384:512]).then_inc(s_xb, 1)

            def row_sum(k, s):
                dve.wait_ge(s_exp, k + 1)
                link(nc.vector.tensor_reduce(rsum[:, :], Ex[:, :, :], AX.X, ALU.add), s_sum, k + 1)
                after(dve, s_pn, k - 1)
                nc.vector.reciprocal(rrec[s][:, :], rsum[:, :]).then_inc(s_rec, 1)

            def residual(k):
                dve.wait_ge(s_o, k + 1)
                h = hT[:, at(k * 2, 2), :].rearrange("p r t -> p (r t)")
                nc.vector.tensor_tensor(h, h, psO, ALU.add).then_inc(s_res, 1)

            def step(k, s, _):
                if runs(k + 1):
                    max_sub(k + 1)
                    evac_xb(k + 1, 1 - s)
                    row_sum(k + 1, 1 - s)
                if runs(k - 1):
                    residual(k - 1)

            steps(dve, -2, NSTEP, 1, LOOP_END, step)
            dve.wait_ge(s_res, NSTEP)
            layernorm(1)

            dve.wait_ge(s_bdload, 48)
            split3(bdrow[:, :], bdrest[:, :], bdmid[:, :], bd3[:, :], s_bd, 0)
            dve.wait_ge(s_rank, E)
            rk = rank[:, :].unsqueeze(1).to_broadcast([P, 3, E])
            bgv = bg_sb[:, :].unsqueeze(1).to_broadcast([P, 3, E])
            dve.wait_ge(s_fload, 96)

            def wide(v):
                return v.unsqueeze(2).to_broadcast([P, 3, E])

            def fstep(k, s, h):
                n = k + 1
                dve.wait_ge(s_lg, n)
                link(nc.vector.tensor_tensor(lg[:, :, :], psL[s].rearrange("p (j e) -> p j e", e=E), bgv, ALU.add), s_lgb, n)
                link(nc.vector.tensor_reduce(lmax[:, :], lg[:, :, :], AX.X, ALU.max), s_lmax, n)
                link(nc.vector.tensor_tensor(ld[:, :, :], lg[:, :, :], wide(lmax[:, :]), ALU.subtract), s_lsub, n)
                link(nc.vector.scalar_tensor_tensor(out=lscore[:, :, :], in0=ld[:, :, :], scalar=0.0, in1=rk,
                                                    op0=ALU.is_equal, op1=ALU.mult), s_lscore, n)
                link(nc.vector.tensor_reduce(lbest[:, :], lscore[:, :, :], AX.X, ALU.max), s_lbest, n)
                nc.vector.tensor_tensor(lmask[:, :, :], lscore[:, :, :], wide(lbest[:, :]), ALU.is_equal).then_inc(s_lmask, 1)
                dve.wait_ge(s_gexp, n)
                link(nc.vector.tensor_reduce(lsum[:, :], le[:, :, :], AX.X, ALU.add), s_lsum, n)
                link(nc.vector.reciprocal(lrec[:, :], lsum[:, :]), s_lrec, n)
                dve.wait_ge(s_lmask, n)
                link(nc.vector.tensor_tensor(gate[:, :, :], lmask[:, :, :], wide(lrec[:, :]), ALU.mult), s_gate, n)
                for j in range(3):
                    dve.wait_ge(s_y, k * 3 + (j + 1))
                    link(nc.vector.tensor_tensor(z[:, j % 2, :, :], psY[j].rearrange("p (e c) -> p e c", e=E),
                                                 gate[:, j, :].unsqueeze(2).to_broadcast([P, E, F]), ALU.mult),
                         s_z, k * 3 + (j + 1))
                    nc.vector.tensor_reduce(ysel[:, j, :], z[:, j % 2, :, :].rearrange("p e c -> p c e"), AX.X,
                                            ALU.add).then_inc(s_ys, 1)
                dve.wait_ge(s_ys, k * 3 + 3)
                after(dve, s_out[s], h * 32)
                nc.vector.tensor_tensor(osb[s][:, :, :], ysel[:, :, :], psR[s].rearrange("p (j c) -> p j c", j=3),
                                        ALU.add).then_inc(s_fin, 1)

            steps(dve, 0, NF - 1, 2, NF - 1, fstep)

        @block.tensor
        def _(pe):
            mm = nc.tensor.matmul
            def score(hf):
                for i in range(HALF):
                    pair = hf * HALF + i
                    if pair % (NPAIR // NX) == 0:
                        pe.wait_ge(s_x[pair // (NPAIR // NX)], 16)
                    last = mm(psScore[hf], wscore[:, i * 96:i * 96 + 96], x_sb[:, pair, :], start=(i == 0), stop=(i == HALF - 1))
                last.then_inc(s_score, 1)

            pe.wait_ge(s_wsc, 5)
            score(0)
            pe.wait_ge(s_aload, ALOADS)
            for h in range(H):
                last = mm(psMM[:, h * F:(h + 1) * F], k_sb[:, h, :], q_sb[:, h, :], start=True, stop=True)
            last.then_inc(s_mm, 1)
            score(1)

            pe.wait_ge(s_sel, 3)
            for hf in range(2):
                pe.wait_ge(s_wpc, 5 * (hf + 1))

                def broadcast(j, s, _):
                    after(pe, s_prod, j - 1)
                    mm(psW[s], sel[:, at(j - hf * HALF, 1), :].rearrange("q o m -> q (o m)"), wpieces[:, hf, :],
                       start=True, stop=True).then_inc(s_wbc, 1)

                lo = hf * HALF + (2 if hf == 0 else 0)
                steps(pe, hf * HALF, (hf + 1) * HALF - 1, lo, (hf + 1) * HALF - 1, broadcast)

            def layernorm(n):
                for c in range(NLN):
                    mm(psLN[c], mean64[:, :], hT[:, c * LNC:(c + 1) * LNC, :].rearrange("p r t -> p (r t)"),
                       start=True, stop=True).then_inc(s_mean, 1)
                for c in range(NLN):
                    pe.wait_ge(s_sq, n * NLN + c + 1)
                    mm(psLN[c], mean64[:, :], sq[:, c, :], start=True, stop=True).then_inc(s_var, 1)

            pe.wait_ge(s_zero, 1)
            pe.wait_ge(s_mmc, 1)
            pe.wait_ge(s_pool, NPAIR)
            layernorm(0)

            def make_g(k, s, h):
                pe.wait_ge(s_xt[s], h * 64 + 64)
                after(pe, s_gev, k)
                after(pe, s_res, k - 3)
                for c in range(HC):
                    last = mm(psG[:, c // 2, (c % 2) * G4:(c % 2 + 1) * G4], MM[:, c, :], XT[s][0:F, :, 0:NW],
                              start=True, stop=True)
                last.then_inc(s_g, 1)

            def scores(k, s):
                pe.wait_ge(s_gev, k + 1)
                after(pe, s_sub, k)
                after(pe, s_xb, k * 2)
                for b in range(4):
                    last = mm(psS[:, b // 2, (b % 2) * G4:(b % 2 + 1) * G4], XT[s][:, b, :],
                              G[s][:, :, b * NW:(b + 1) * NW], start=True, stop=True)
                last.then_inc(s_s, 1)

            def transpose_x(k, s):
                after(pe, s_cev, k - 1)
                for b in range(4):
                    bk = psS if b < 2 else psC
                    last = nc.tensor.transpose(bk[:, b % 2, 384:512], XT[s][:, b, :], ident[:, :])
                last.then_inc(s_xtr, 1)

            def transpose_p(k, s):
                pe.wait_ge(s_pn, k + 1)
                after(pe, s_pt, k)
                for b in range(4):
                    for cc in range(2):
                        g = (b % 2) * 2 + cc
                        last = nc.tensor.transpose(psT[:, b // 2, g * P:(g + 1) * P],
                                                   Pn[s][:, b * 4 + 2 * cc:b * 4 + 2 * cc + 2, :].rearrange("p c u -> p (c u)"),
                                                   ident[:, :])
                last.then_inc(s_t, 1)

            def context(k, s):
                pe.wait_ge(s_pt, k + 1)
                pe.wait_ge(s_xb, k * 2 + (4 if runs(k + 1) else 2))
                after(pe, s_cev, k)
                for b in range(4):
                    last = mm(psC[:, b // 2, (b % 2) * G4:(b % 2 + 1) * G4], XB[s][:, b, :], PT[:, b, :],
                              start=True, stop=True)
                last.then_inc(s_c, 1)

            def project(k):
                pe.wait_ge(s_cev, k + 1)
                after(pe, s_res, k)
                pe.wait_ge(s_gev, k + 4 if runs(k + 3) else NSTEP)
                for b2 in range(2):
                    for g in range(4):
                        last = mm(psO, VOz[:, b2, g, :], C[:, :, g, :].rearrange("p (r b) t -> p r b t", b=2)[:, :, b2, :],
                                  start=(b2 == 0 and g == 0), stop=(b2 == 1 and g == 3))
                last.then_inc(s_o, 1)

            def step(k, s, h):
                if runs(k + 1):
                    scores(k + 1, 1 - s)
                    transpose_x(k + 1, 1 - s)
                if runs(k + 2):
                    make_g(k + 2, s, h + 1)
                if runs(k):
                    transpose_p(k, s)
                if runs(k - 1):
                    project(k - 1)
                if runs(k):
                    context(k, s)

            pe.wait_ge(s_idt, 1)
            steps(pe, -2, NSTEP, 1, LOOP_END, step)
            pe.wait_ge(s_res, NSTEP)
            layernorm(1)

            pe.wait_ge(s_fload, 96)
            pe.wait_ge(s_bd, 5)

            def hidden(k, s, h):
                pe.wait_ge(s_xq[s], h * 64 + 64)
                after(pe, s_gelu, k * 2)
                for c in range(HCH):
                    last = mm(psH[c], w1_sb[:, c * P:(c + 1) * P], xq[s][0:F, :], start=True, stop=True)
                last.then_inc(s_h, 1)

            def gates(k, s):
                pe.wait_ge(s_gelu, k * 2 + 2)
                after(pe, s_fin, k - 1)
                for j, t0 in enumerate(STARTS):
                    for c in range(HCH):
                        mm(psL[s][:, j * E:(j + 1) * E], Hs[s][:, c, t0:t0 + P], wg_sb[:, c, :],
                           start=(c == 0), stop=(c == HCH - 1))
                for j, t0 in enumerate(STARTS):
                    last = mm(psR[s][:, j * F:(j + 1) * F], xq[s][F:2 * F, t0:t0 + P], ident[F:2 * F, F:2 * F],
                              start=True, stop=True)
                last.then_inc(s_lg, 1)

            def experts(k, s):
                for j, t0 in enumerate(STARTS):
                    after(pe, s_z, k * 3 + (j - 2))
                    for c in range(HCH):
                        mm(psY[j], Hs[s][:, c, t0:t0 + P], wd_sb[:, c, :, :].rearrange("p e c -> p (e c)"),
                           start=(c == 0), stop=False)
                    mm(psY[j], ones3[:, :], bd3[:, :], start=False, stop=True).then_inc(s_y, 1)

            def fstep(k, s, h):
                gates(k, s)
                if runs(k + 1, NF):
                    hidden(k + 1, 1 - s, h + s)
                experts(k, s)

            hidden(0, 0, 0)
            steps(pe, 0, NF - 1, 1, NF - 2, fstep)


_INS = ['x','L0_tok_w','L0_tok_b','L0_attn_Q','L0_attn_K','L0_attn_VO','L0_ffn_W1','L0_ffn_b1','L0_ffn_Wg','L0_ffn_bg','L0_ffn_Wd','L0_ffn_bd']
_OUTS = [((64, 47, 64), 'float32')]


def kernel(**inputs):
    import numpy as _np
    import concourse.bacc as _bacc
    from concourse import mybir as _mybir
    from concourse.bass_utils import run_bass_kernel_spmd as _run

    nc = _bacc.Bacc("TRN2", target_bir_lowering=False, num_devices=1)
    arrays, args = {}, []
    for name in _INS:
        a = _np.ascontiguousarray(inputs[name])
        arrays[f"in_{name}_dram"] = a
        args.append(nc.dram_tensor(f"in_{name}_dram", a.shape, _mybir.dt.from_np(a.dtype), kind="ExternalInput").ap())
    for i, (shape, dtype) in enumerate(_OUTS):
        dt = _mybir.dt.from_np(_np.dtype(dtype))
        args.append(nc.dram_tensor(f"out_{i}_dram", shape, dt, kind="ExternalOutput").ap())
    audio_tower_kernel(nc, *args)
    r = _run(nc, [arrays], core_ids=[0])
    got = tuple(r.results[0][f"out_{i}_dram"] for i in range(len(_OUTS)))
    return got[0]
```

```python
from contextlib import ExitStack

import concourse.bass as bass
from concourse import mybir

F32 = mybir.dt.float32
F32R = mybir.dt.float32r
I32 = mybir.dt.int32
BF16 = mybir.dt.bfloat16
ALU = mybir.AluOpType
ACT = mybir.ActivationFunctionType
AX = mybir.AxisListType


def audio_tower_kernel(nc, x, tok_w, tok_b, Q, K, VO, W1, b1, Wg, bg, Wd, bd, out):
    B, F, T_RAW = x.shape
    WIN = 8
    NW = -(-T_RAW // WIN)
    T = NW * WIN
    H, R, _ = Q.shape
    HID = W1.shape[1]
    E = Wg.shape[1]
    NPAIR = B // 2
    P = 128
    TP = 64
    NQ = 4
    QP = NPAIR // NQ
    NR = QP // 2
    HC = H // 2
    LNW = QP * NW
    NSTEP = NPAIR // 2
    G4 = 4 * NW
    QS = NSTEP // NQ
    NF = 8
    FT = 8 * NW
    HCH = HID // P
    STARTS = [0, P, FT - P]
    SKIP = 2 * P - (FT - P)
    EC = E * F
    EPS = 1e-5
    COARSE = -(1 << 12)

    with ExitStack() as ctx:
        def sb(name, shape, dt=F32):
            return ctx.enter_context(nc.sbuf_tensor(name, shape, dt))

        def ps(name, shape):
            return ctx.enter_context(nc.psum_tensor(name, shape, F32))

        def sem(name):
            return ctx.enter_context(nc.semaphore(name))

        x_sb = sb("x_sb", [P, NPAIR, T])
        wcol = sb("wcol", [P, 1])
        eps = sb("eps", [P, 1])
        tokb = sb("tokb", [P, 1])
        wscore = sb("wscore", [P, QP * (96 + 2)])
        sel = sb("sel", [96, QP, P], BF16)
        ident = sb("ident", [P, P])
        mean64 = sb("mean64", [P, P])
        ones3 = sb("ones3", [96, P], BF16)
        wmax = sb("wmax", [96, NW])
        wmaxb = sb("wmaxb", [96, NW])
        wexp = sb("wexp", [96, NQ, T])
        wsum = sb("wsum", [96, NW])
        wrec = sb("wrec", [96, NW])
        wprob = sb("wprob", [96, T])
        wrest = sb("wrest", [96, T])
        wmid = sb("wmid", [96, T], BF16)
        wpieces = sb("wpieces", [96, T], BF16)
        wbc = sb("wbc", [P, 2, 2, T])
        prod = sb("prod", [P, 2, 2, T])
        hT = sb("hT", [P, NPAIR, NW])
        xnT = sb("xnT", [P, NPAIR, NW])
        xn_coarse = sb("xn_coarse", [P, NPAIR, NW])
        xn_fine = sb("xn_fine", [P, NPAIR, NW])
        cen = sb("cen", [P, LNW])
        sq = sb("sq", [P, LNW])
        lnv = sb("lnv", [P, LNW])
        rstd = sb("rstd", [P, LNW])
        q_sb = sb("q_sb", [R, H, F])
        k_sb = sb("k_sb", [R, H, 2, F])
        XG = [sb(f"XG{s}", [P, 4, NW], F32R) for s in range(2)]
        mm_coarse = sb("mm_coarse", [P, HC * P], F32R)
        mm_fine = sb("mm_fine", [P, HC * P], F32R)
        VOg = sb("VOg", [P, 4, F])
        XT = [sb(f"XT{s}", [P, 4, P]) for s in range(2)]
        XB = [sb(f"XB{s}", [P, 4, P]) for s in range(2)]
        G = [sb(f"G{s}", [P, HC, G4]) for s in range(2)]
        rmax = sb("rmax", [P, 16])
        D = sb("D", [P, 16, NW])
        Ex = sb("Ex", [P, 16, NW])
        rsum = sb("rsum", [P, 16])
        rrec = [sb(f"rrec{s}", [P, 16]) for s in range(2)]
        Pn = [sb(f"Pn{s}", [P, 16, TP]) for s in range(2)]
        PT = sb("PT", [P, 4, G4])
        C = sb("C", [P, 4, 4, NW])
        w1_sb = sb("w1_sb", [P, HID])
        w1_coarse = sb("w1_coarse", [P, HID], F32R)
        w1_fine = sb("w1_fine", [P, HID], F32R)
        b1_sb = sb("b1_sb", [P, HCH])
        wg_sb = sb("wg_sb", [P, HCH, E])
        bg_sb = sb("bg_sb", [P, E])
        wd_sb = sb("wd_sb", [P, HCH, E, F])
        w_bits = sb("w_bits", [P, HCH * EC], I32)
        wd_coarse = sb("wd_coarse", [P, HCH, EC], F32R)
        wd_fine = sb("wd_fine", [P, HCH, EC], F32R)
        bdrow = sb("bdrow", [96, EC])
        bdrest = sb("bdrest", [96, EC])
        bdmid = sb("bdmid", [96, EC], BF16)
        bd3 = sb("bd3", [96, EC], BF16)
        rank = sb("rank", [P, E])
        hq = [sb(f"hq{s}", [F, FT]) for s in range(2)]
        xq = [sb(f"xq{s}", [P, FT], F32R) for s in range(2)]
        Hs = [sb(f"Hs{s}", [P, HCH, FT]) for s in range(2)]
        h_coarse = [sb(f"h_coarse{s}", [P, HCH, FT], F32R) for s in range(2)]
        h_fine = [sb(f"h_fine{s}", [P, HCH, FT], F32R) for s in range(2)]
        lg = sb("lg", [P, 3, E])
        lmax = sb("lmax", [P, 3])
        ld = sb("ld", [P, 3, E])
        le = sb("le", [P, 3, E])
        lsum = sb("lsum", [P, 3])
        lrec = sb("lrec", [P, 3])
        lscore = sb("lscore", [P, 3, E])
        lbest = sb("lbest", [P, 3])
        lmask = sb("lmask", [P, 3, E])
        gate = sb("gate", [P, 3, E])
        z = sb("z", [P, 2, E, F])
        ysel = sb("ysel", [P, 3, F])
        osb = [sb(f"osb{s}", [P, 3, F]) for s in range(2)]

        bank = ps("bank", [P, 8, 512])

        psScore = [bank[0:96, i, 0:T] for i in range(NQ)]
        psMM = bank[:, 4, :]
        psW = bank[:, 6:8, 0:T]
        psLN = bank[:, 7, 0:LNW]
        psG = bank[:, 0:2, :]
        psT = bank[:, 0:2, :]
        psS = bank[:, 2:4, :]
        psO = bank[:, 2, 0:2 * NW]
        psC = bank[:, 4:6, :]
        psH = [bank[:, i, 0:FT] for i in (0, 1)]
        psL = [bank[:, i, 0:3 * E] for i in (2, 3)]
        psR = [bank[:, i, 64:64 + 3 * F] for i in (2, 3)]
        psY = [bank[:, i, :] for i in (4, 5, 6)]

        NX = 8
        s_x = [sem(f"s_x{i}") for i in range(NX)]
        s_wload = sem("s_wload")
        s_aload = sem("s_aload")
        s_fload = sem("s_fload")
        s_bdload = sem("s_bdload")
        ALOADS = 16 * (3 + 4)
        FLOADS = 16 * (5 + HCH)
        s_zero = sem("s_zero")
        s_vz = sem("s_vz")
        s_pz = sem("s_pz")
        s_sel = sem("s_sel")
        s_idt = sem("s_idt")
        s_wsc = sem("s_wsc")
        s_rank = sem("s_rank")
        s_score = sem("s_score")
        s_wmax, s_wmaxb, s_wsub, s_wexp, s_wsum, s_wrec, s_wprob = [
            sem(n) for n in ("s_wmax", "s_wmaxb", "s_wsub", "s_wexp", "s_wsum", "s_wrec", "s_wprob")]
        s_wpc = sem("s_wpc")
        s_wbc = sem("s_wbc")
        s_wcp = sem("s_wcp")
        s_prod = sem("s_prod")
        s_prodp = sem("s_prodp")
        s_pool = sem("s_pool")
        s_mm = sem("s_mm")
        s_mmc = sem("s_mmc")
        s_mmb = sem("s_mmb")
        s_wbits = sem("s_wbits")
        s_wparts = sem("s_wparts")
        s_mean = sem("s_mean")
        s_cen = sem("s_cen")
        s_sq = sem("s_sq")
        s_var = sem("s_var")
        s_ln = sem("s_ln")
        s_rstd = sem("s_rstd")
        s_nrm = sem("s_nrm")
        s_crs = sem("s_crs")
        s_xn = sem("s_xn")
        s_xt = [sem(f"s_xt{i}") for i in range(2)]
        s_xg = [sem(f"s_xg{i}") for i in range(2)]
        s_g = sem("s_g")
        s_gev = sem("s_gev")
        s_s = sem("s_s")
        s_xtr = sem("s_xtr")
        s_xb = sem("s_xb")
        s_max = sem("s_max")
        s_sub = sem("s_sub")
        s_exp = sem("s_exp")
        s_sum = sem("s_sum")
        s_rec = sem("s_rec")
        s_pn = sem("s_pn")
        s_t = sem("s_t")
        s_pt = sem("s_pt")
        s_c = sem("s_c")
        s_cev = sem("s_cev")
        s_o = sem("s_o")
        s_res = sem("s_res")
        s_bd = sem("s_bd")
        s_xq = [sem(f"s_xq{i}") for i in range(2)]
        s_h = sem("s_h")
        s_gelu = sem("s_gelu")
        s_hc = sem("s_hc")
        s_hf = sem("s_hf")
        s_lg = sem("s_lg")
        s_y = sem("s_y")
        s_lgb, s_lmax, s_lsub, s_gexp, s_lsum, s_lrec, s_lscore, s_lbest, s_lmask, s_gate = [
            sem(n) for n in ("s_lgb", "s_lmax", "s_lsub", "s_gexp", "s_lsum", "s_lrec", "s_lscore", "s_lbest",
                             "s_lmask", "s_gate")]
        s_z = sem("s_z")
        s_ys = sem("s_ys")
        s_fin = sem("s_fin")
        s_out = [sem(f"s_out{i}") for i in range(2)]

        def after(eng, s, v):
            if not isinstance(v, int) or v > 0:
                eng.wait_ge(s, v)

        def steps(eng, first, last, lo, hi, body):
            for k in range(first, lo):
                body(k, k % 2, k // 2)
            if hi > lo:
                assert (hi + 1 - lo) % 2 == 0
                with eng.Fori(0, (hi + 1 - lo) // 2) as i:
                    for s in range(lo, lo + 2):
                        body(i * 2 + s, s % 2, i + s // 2)
            for k in range(max(hi, lo - 1) + 1, last + 1):
                body(k, k % 2, k // 2)

        def attention_steps(eng, step):
            step(-2, 0, 1, 1)
            step(-1, 1, 1, 2)
            step(0, 0, 1, 3)
            with eng.Fori(2, NQ) as q:
                for j in range(QS):
                    step(q * QS + (j + 1 - 2 * QS), (j + 1) % 2, q, j)
            for k in range(2 * QS + 1, NSTEP + 1):
                step(k, k % 2, *{9: (0, 4), 10: (1, 4), 13: (2, 4)}.get(k, (None, None)))

        def runs(k, n=NSTEP):
            return not isinstance(k, int) or 0 <= k < n

        def at(k, n):
            return slice(k, k + n) if isinstance(k, int) else bass.ds(k, n)

        block = ctx.enter_context(nc.Block())

        @block.sync
        def _(sp):
            xv = x.rearrange("(p b) f t -> (b f) p t", b=2)
            per = NPAIR // NX
            for b2 in range(2):
                sp.dma_start(wcol[b2 * F:b2 * F + F, :], tok_w.rearrange("o f -> f o")).then_inc(s_wload, 16)
            for i in range(NX):
                sp.dma_start(x_sb[:, i * per:(i + 1) * per, 0:T_RAW], xv[:, i * per:(i + 1) * per, :]).then_inc(s_x[i], 16)

            def load_x(k, s):
                after(sp, s_xtr, k - 1)
                for half, src in enumerate((xn_coarse, xn_fine)):
                    dst = XG[s][half * F:half * F + F, :, :].bitcast(F32).rearrange("p (r b) t -> p r b t", b=2)
                    for b2 in range(2):
                        sp.dma_start(dst[:, :, b2, :], src[b2 * F:b2 * F + F, at(k * 2, 2), :]).then_inc(s_xg[s], 16)
                dst = XT[s][:, :, :].rearrange("p (r b) c -> p r b c", b=2)
                for b2 in range(2):
                    for par in range(2):
                        sp.dma_start(dst[par * TP:par * TP + F, :, b2, par * TP:par * TP + NW],
                                     xnT[b2 * F:b2 * F + F, at(k * 2, 2), :]).then_inc(s_xt[s], 16)

            sp.wait_ge(s_zero, 1)
            sp.wait_ge(s_xn, 1)
            for k in range(QS):
                load_x(k, k % 2)
            with sp.Fori(1, NQ) as q:
                sp.wait_ge(s_xn, q + 1)
                for j in range(QS):
                    load_x(q * QS + j, j % 2)

            def load_xq(k, s, h):
                sp.wait_ge(s_xn, h + (NQ + 1))
                after(sp, s_lg, k - 1)
                for to, src in ((xq[s][0:F, :].bitcast(F32), xn_coarse), (xq[s][F:P, :].bitcast(F32), xn_fine),
                                (hq[s][:, :], hT)):
                    dst = to.rearrange("p (r b t) -> p r b t", b=2, t=NW)
                    for b2 in range(2):
                        sp.dma_start(dst[:, :, b2, :], src[b2 * F:b2 * F + F, at(k * 4, 4), :]).then_inc(s_xq[s], 16)

            steps(sp, 0, NF - 1, 2, NF - 1, load_xq)

        @block.gpsimd
        def _(pool):
            pool.memset(ident[:, :], 0.0).then_inc(s_pz, 1)
            pool.memset(sel[:, :, :], 0.0).then_inc(s_pz, 1)
            pool.wait_ge(s_pz, 2)
            pool.affine_select(out=ident[:, :], in_=ident[:, :], compare_op=ALU.not_equal, fill=1.0,
                               base=0, pattern=[[-1, P]], channel_multiplier=1).then_inc(s_idt, 1)
            for j in range(3):
                pool.wait_ge(s_idt if j == 0 else s_sel, max(j, 1))
                v = sel[32 * j:32 * j + 32, :, :].rearrange("q i (b f) -> q i b f", b=2)
                pool.affine_select(out=v, in_=v, compare_op=ALU.not_equal, fill=1.0, base=0,
                                   pattern=[[-2, QP], [-1, 2], [0, F]], channel_multiplier=1).then_inc(s_sel, 1)
            pool.wait_ge(s_sel, 3)
            for s in range(2):
                pool.memset(Pn[s][:, :, :], 0.0).then_inc(s_pz, 1)
            pool.wait_ge(s_pz, 4)
            for e in range(E):
                pool.memset(rank[:, e:e + 1], float(E - e)).then_inc(s_rank, 1)

            def round_products(n, s, direct=0):
                pool.wait_ge(s_wcp, n + 1)
                after(pool, s_pool, n - 1)
                pool.tensor_tensor(prod[:, s, direct:2, :], x_sb[:, at(n * 2 + direct, 2 - direct), :],
                                   wbc[:, s, direct:2, :], ALU.mult).then_inc(s_prodp, 1)

            def normalise(k, s):
                pool.wait_ge(s_rec, k + 1)
                after(pool, s_t, k - 1)
                pool.tensor_tensor(Pn[s][:, :, 0:NW], Ex[:, :, :],
                                   rrec[s][:, :].unsqueeze(2).to_broadcast([P, 16, NW]),
                                   ALU.mult).then_inc(s_pn, 1)

            def step(k, s, q=None, slot=None):
                if slot in (1, 2):
                    round_products(q * NR + 2 * (slot - 1), 0)
                if runs(k + 1):
                    normalise(k + 1, 1 - s)
                if slot in (1, 2):
                    round_products(q * NR + 2 * (slot - 1) + 1, 1)

            for n in range(NR):
                round_products(n, n % 2, direct=1)
            attention_steps(pool, step)

            def fine_hidden(k, s):
                pool.wait_ge(s_hc, k + 1)
                after(pool, s_y, 3 * (k - 1))
                pool.tensor_tensor(h_fine[s][:, :, :], Hs[s][:, :, :], h_coarse[s][:, :, :], ALU.subtract).then_inc(s_hf, 1)

            def store(k, s, _):
                if runs(k + 1, NF):
                    fine_hidden(k + 1, 1 - s)
                pool.wait_ge(s_fin, k + 1)
                o = out.rearrange("b t c -> (b t) c")[at(k * FT, FT), :]
                pool.dma_start(o[0:2 * P, :].rearrange("(j p) c -> p j c", p=P), osb[s][:, 0:2, :]).then_inc(s_out[s], 16)
                pool.dma_start(o[2 * P:FT, :], osb[s][SKIP:P, 2, :]).then_inc(s_out[s], 16)

            fine_hidden(0, 0)
            steps(pool, 0, NF - 1, 1, NF - 2, store)
            for s in range(2):
                pool.wait_ge(s_out[s], 32 * (NF // 2))

        @block.scalar
        def _(act):
            act.preload_act_table_set("natural_log_exp_and_others")
            act.dma_start(tokb[:, :], tok_b.rearrange("(o a) -> o a", a=1).to_broadcast([P, 1])).then_inc(s_wload, 16)
            act.dma_start(q_sb[:, :, :], Q.rearrange("h r d -> r h d")).then_inc(s_aload, 16)
            for copy in range(2):
                act.dma_start(k_sb[:, :, copy, :], K.rearrange("h r d -> r h d")).then_inc(s_aload, 16)
            vov = VO.rearrange("(cc c2 par) d e -> c2 d cc par e", c2=2, par=2)
            for c2 in range(2):
                for cc in range(2):
                    act.dma_start(VOg[c2 * F:c2 * F + F, 2 * cc:2 * cc + 2, :], vov[c2, :, cc]).then_inc(s_aload, 16)
            for half in range(2):
                act.dma_start(w1_sb[half * F:half * F + F, :], W1).then_inc(s_fload, 16)
            act.dma_start(b1_sb[:, :], b1.rearrange("(c p) -> p c", p=P), allow_slow_non_contiguous=True).then_inc(s_fload, 16)
            act.dma_start(wg_sb[:, :, :], Wg.rearrange("(c p) e -> p c e", p=P)).then_inc(s_fload, 16)
            act.dma_start(bg_sb[:, :], bg.rearrange("(o e) -> o e", o=1).to_broadcast([P, E])).then_inc(s_fload, 16)
            for c in range(HCH):
                act.dma_start(wd_sb[:, c, :, :], Wd[:, c * P:(c + 1) * P, :].rearrange("e p c -> p e c")).then_inc(s_fload, 16)
            act.wait_ge(s_vz, 4)
            for j in range(3):
                act.dma_start(bdrow[32 * j:32 * j + 1, :], bd.rearrange("(o e) c -> o (e c)", o=1)).then_inc(s_bdload, 16)

            def window_exp(q):
                act.wait_ge(s_wsub, q + 1)
                nc.scalar.activation(wexp[:, q, :], wexp[:, q, :], ACT.Exp).then_inc(s_wexp, 1)

            def copy_weights(n, s, direct=0):
                act.wait_ge(s_wbc, n + 1)
                after(act, s_prodp, n - 1)
                nc.scalar.copy(wbc[:, s, direct:2, :], psW[:, direct:2, :]).then_inc(s_wcp, 1)

            def square(n):
                act.wait_ge(s_cen, n + 1)
                nc.scalar.activation(sq[:, :], cen[:, :], ACT.Square).then_inc(s_sq, 1)

            def inverse_root(n):
                act.wait_ge(s_var, n + 1)
                nc.scalar.activation(lnv[:, :], psLN, ACT.Ln, bias=eps[:, 0:1]).then_inc(s_ln, 1)
                act.wait_ge(s_ln, n + 1)
                nc.scalar.activation(rstd[:, :], lnv[:, :], ACT.Exp, scale=-0.5).then_inc(s_rstd, 1)

            def evac_g(k, s):
                after(act, s_s, k - 1)
                for a in range(2):
                    act.wait_ge(s_g, k * 2 + (a + 1))
                    nc.scalar.copy(G[s][:, 2 * a:2 * a + 2, :].rearrange("p c n -> p (c n)"), psG[:, a, 0:2 * G4]).then_inc(s_gev, 1)

            def exp(k):
                act.wait_ge(s_sub, k + 1)
                after(act, s_pn, k)
                nc.scalar.activation(Ex[:, :, :], D[:, :, :], ACT.Exp, scale=float(F) ** -0.5).then_inc(s_exp, 1)

            def evac_t(k):
                act.wait_ge(s_t, k + 1)
                after(act, s_c, k)
                nc.scalar.copy(PT[:, :, :].rearrange("p b (g t) -> p (b g) t", t=NW),
                               psT.rearrange("p k (g t) -> p (k g) t", t=TP)[:, :, 0:NW]).then_inc(s_pt, 1)

            def evac_c(k):
                act.wait_ge(s_c, k + 1)
                after(act, s_o, k)
                nc.scalar.copy(C[:, :, :, :].rearrange("p (k b) g t -> p k b (g t)", k=2),
                               psC[:, :, 0:2 * G4].rearrange("p k (b n) -> p k b n", b=2)).then_inc(s_cev, 1)

            def step(k, s, q=None, slot=None):
                ln = q + NQ if slot == 4 else q
                if runs(k + 2):
                    evac_g(k + 2, s)
                if runs(k + 1):
                    exp(k + 1)
                if runs(k):
                    evac_t(k)
                if slot == 1 or slot == 2:
                    copy_weights(q * NR + 2 * (slot - 1), 0)
                if slot == 3 or slot == 4:
                    square(ln)
                if runs(k):
                    evac_c(k)
                if slot == 1 or slot == 2:
                    copy_weights(q * NR + 2 * (slot - 1) + 1, 1)
                if slot == 3 or slot == 4:
                    inverse_root(ln)

            window_exp(0)
            window_exp(1)
            for n in range(NR):
                copy_weights(n, n % 2, direct=1)
            square(0)
            inverse_root(0)
            window_exp(2)
            window_exp(3)
            attention_steps(act, step)
            square(2 * NQ - 1)
            inverse_root(2 * NQ - 1)

            def gelu(k, s):
                act.wait_ge(s_h, k + 1)
                after(act, s_y, 3 * (k - 1))
                for c in range(HCH):
                    nc.scalar.activation(Hs[s][:, c, :], psH[c], ACT.Gelu, bias=b1_sb[:, c:c + 1]).then_inc(s_gelu, 1)

            def gate_exp(k):
                act.wait_ge(s_lsub, k + 1)
                nc.scalar.activation(le[:, :, :], ld[:, :, :], ACT.Exp).then_inc(s_gexp, 1)

            def coarse_hidden(k, s):
                act.wait_ge(s_gelu, k * 2 + 2)
                after(act, s_y, 3 * (k - 1))
                nc.scalar.copy(h_coarse[s][:, :, :], Hs[s][:, :, :]).then_inc(s_hc, 1)

            act.wait_ge(s_fload, FLOADS)
            act.preload_act_table_set("gelu_and_others")
            gelu(0, 0)
            coarse_hidden(0, 0)

            def fstep(k, s, _):
                act.preload_act_table_set("exp_and_others")
                gate_exp(k)
                if runs(k + 1, NF):
                    act.preload_act_table_set("gelu_and_others")
                    gelu(k + 1, 1 - s)
                    coarse_hidden(k + 1, 1 - s)

            steps(act, 0, NF - 1, 1, NF - 2, fstep)

        @block.vector
        def _(dve):
            def link(ins, s, n):
                ins.then_inc(s, 1)
                dve.wait_ge(s, n)

            def split3(src, rest, mid, pieces, s, n):
                link(nc.vector.tensor_copy(pieces, src), s, n + 1)
                link(nc.vector.tensor_tensor(rest, src, pieces, ALU.subtract), s, n + 2)
                link(nc.vector.tensor_copy(mid, rest), s, n + 3)
                link(nc.vector.tensor_copy(pieces[32:64], mid[32:64]), s, n + 4)
                link(nc.vector.tensor_tensor(pieces[64:96], rest[64:96], mid[64:96], ALU.subtract), s, n + 5)

            def coarse(bits, v):
                return nc.vector.tensor_scalar(bits, v.bitcast(I32), COARSE, None, ALU.bitwise_and)

            nc.vector.memset(wscore[:, :], 0.0).then_inc(s_wsc, 1)
            nc.vector.memset(x_sb[:, :, T_RAW:T], 0.0).then_inc(s_wsc, 1)
            nc.vector.memset(eps[:, :], EPS).then_inc(s_wsc, 1)
            dve.wait_ge(s_wsc, 3)
            dve.wait_ge(s_wload, 48)
            for b2 in range(2):
                dst = wscore[b2 * F:b2 * F + F, :].rearrange("p (i c) -> p i c", c=98)[:, :, b2:b2 + 65:32]
                nc.vector.tensor_copy(dst, wcol[b2 * F:b2 * F + F, :].unsqueeze(2).to_broadcast([F, QP, 3])).then_inc(s_wsc, 1)
            for v in (XT[0][:, :, :], XT[1][:, :, :]):
                nc.vector.memset(v, 0.0).then_inc(s_vz, 1)
            nc.vector.memset(bdrow[:, :], 0.0).then_inc(s_vz, 1)
            nc.vector.memset(mean64[:, :], 0.0).then_inc(s_vz, 1)
            dve.wait_ge(s_vz, 4)
            for b2 in range(2):
                nc.vector.memset(mean64[b2 * F:b2 * F + F, b2 * F:b2 * F + F], 1.0 / F).then_inc(s_vz, 1)
            dve.wait_ge(s_vz, 6)
            nc.vector.memset(ones3[:, :], 1.0).then_inc(s_zero, 1)

            win = "p (w k) -> p w k"
            def window_max(q):
                n = q + 1
                dve.wait_ge(s_score, n)
                sq_ = psScore[q].rearrange(win, k=WIN)
                link(nc.vector.tensor_reduce(wmax[:, :], sq_, AX.X, ALU.max), s_wmax, n)
                link(nc.vector.tensor_scalar(wmaxb[:, :], wmax[:, :], tokb[0:96, 0:1], None, ALU.add), s_wmaxb, n)
                nc.vector.scalar_tensor_tensor(
                    out=wexp[:, q, :].rearrange(win, k=WIN), in0=sq_, scalar=tokb[0:96, 0:1],
                    in1=wmaxb[:, :].unsqueeze(2).to_broadcast([96, NW, WIN]), op0=ALU.add,
                    op1=ALU.subtract).then_inc(s_wsub, 1)

            def window_weights(q):
                n = q + 1
                dve.wait_ge(s_wexp, n)
                ex = wexp[:, at(q, 1), :].rearrange("p o (w k) -> p (o w) k", k=WIN)
                link(nc.vector.tensor_reduce(wsum[:, :], ex, AX.X, ALU.add), s_wsum, n)
                link(nc.vector.reciprocal(wrec[:, :], wsum[:, :]), s_wrec, n)
                link(nc.vector.tensor_tensor(wprob[:, :].rearrange(win, k=WIN), ex,
                                             wrec[:, :].unsqueeze(2).to_broadcast([96, NW, WIN]), ALU.mult), s_wprob, n)
                after(dve, s_wbc, q * NR)
                split3(wprob[:, :], wrest[:, :], wmid[:, :], wpieces[:, :], s_wpc, q * 5)

            def direct_product(n, s):
                dve.wait_ge(s_wbc, n + 1)
                after(dve, s_pool, n - 1)
                nc.vector.tensor_tensor(prod[:, s, 0, :], x_sb[:, 2 * n, :], psW[:, 0, :], ALU.mult).then_inc(s_prod, 1)

            def pool_round(n, s):
                if isinstance(n, int) and n < NR:
                    dve.wait_ge(s_prod, n + 1)
                dve.wait_ge(s_prodp, n + 1)
                nc.vector.tensor_reduce(hT[:, at(n * 2, 2), :], prod[:, s, :, :].rearrange("p j (w k) -> p j w k", k=WIN),
                                        AX.X, ALU.add).then_inc(s_pool, 1)

            def quarter(t, q):
                return t[:, at(q * QP, QP), :].rearrange("p r t -> p (r t)")

            def centre(n, q):
                dve.wait_ge(s_mean, n + 1)
                nc.vector.tensor_tensor(cen[:, :], quarter(hT, q), psLN, ALU.subtract).then_inc(s_cen, 1)

            def scale(n, q):
                dve.wait_ge(s_rstd, n + 1)
                link(nc.vector.tensor_tensor(quarter(xnT, q), cen[:, :], rstd[:, :], ALU.mult), s_nrm, n + 1)
                link(coarse(quarter(xn_coarse, q).bitcast(I32), quarter(xnT, q)), s_crs, n + 1)
                nc.vector.tensor_tensor(quarter(xn_fine, q), quarter(xnT, q), quarter(xn_coarse, q), ALU.subtract).then_inc(s_xn, 1)

            sS = psS[:, :, 0:2 * G4].rearrange("p k (g u) -> p k g u", u=NW)

            def max_sub(k):
                dve.wait_ge(s_xtr, k + 1)
                link(nc.vector.tensor_reduce(rmax[:, :].rearrange("p (k g) -> p k g", k=2), sS, AX.X, ALU.max), s_max, k + 1)
                after(dve, s_exp, k)
                nc.vector.tensor_tensor(D[:, :, :].rearrange("p (k g) u -> p k g u", k=2), sS,
                                        rmax[:, :].rearrange("p (k g) -> p k g", k=2).unsqueeze(3).to_broadcast([P, 2, 8, NW]),
                                        ALU.subtract).then_inc(s_sub, 1)

            def evac_xb(k, s):
                after(dve, s_c, k - 1)
                nc.vector.tensor_copy(XB[s][:, 0:2, :], psS[:, :, 384:512]).then_inc(s_xb, 1)
                nc.vector.tensor_copy(XB[s][:, 2:4, :], psC[:, :, 384:512]).then_inc(s_xb, 1)

            def row_sum(k, s):
                dve.wait_ge(s_exp, k + 1)
                link(nc.vector.tensor_reduce(rsum[:, :], Ex[:, :, :], AX.X, ALU.add), s_sum, k + 1)
                after(dve, s_pn, k - 1)
                nc.vector.reciprocal(rrec[s][:, :], rsum[:, :]).then_inc(s_rec, 1)

            def residual(k):
                dve.wait_ge(s_o, k + 1)
                h = hT[:, at(k * 2, 2), :].rearrange("p r t -> p (r t)")
                nc.vector.tensor_tensor(h, h, psO, ALU.add).then_inc(s_res, 1)

            def step(k, s, q=None, slot=None):
                ln = q + NQ if slot == 4 else q
                if runs(k + 1):
                    max_sub(k + 1)
                    evac_xb(k + 1, 1 - s)
                if slot == 3:
                    pool_round(q * NR + 3, 1)
                if runs(k + 1):
                    row_sum(k + 1, 1 - s)
                if runs(k - 1):
                    residual(k - 1)
                if slot == 3 or slot == 4:
                    centre(ln, q)
                if slot == 0:
                    window_weights(q)
                if slot == 2:
                    pool_round(q * NR + 1, 1)
                if slot == 1 or slot == 2:
                    pool_round(q * NR + 2 * (slot - 1), 0)
                if slot == 3 or slot == 4:
                    scale(ln, q)

            window_max(0)
            window_weights(0)
            dve.wait_ge(s_mm, 1)
            link(coarse(w_bits[:, 0:HC * P], psMM), s_mmb, 1)
            nc.vector.tensor_copy(mm_coarse[:, :], w_bits[:, 0:HC * P].bitcast(F32)).then_inc(s_mmc, 1)
            nc.vector.tensor_tensor(mm_fine[:, :], psMM, w_bits[:, 0:HC * P].bitcast(F32), ALU.subtract).then_inc(s_mmc, 1)
            window_max(1)
            direct_product(0, 0)
            direct_product(1, 1)
            pool_round(0, 0)
            direct_product(2, 0)
            pool_round(1, 1)
            direct_product(3, 1)
            pool_round(2, 0)
            pool_round(3, 1)
            centre(0, 0)
            window_weights(1)
            scale(0, 0)
            window_max(2)
            window_max(3)
            dve.wait_ge(s_fload, FLOADS)
            for n, (w, c, f) in enumerate(((w1_sb[:, :], w1_coarse[:, :], w1_fine[:, :]),
                                           (wd_sb[:, :, :, :].rearrange("p c e f -> p (c e f)"),
                                            wd_coarse[:, :, :].rearrange("p c m -> p (c m)"),
                                            wd_fine[:, :, :].rearrange("p c m -> p (c m)")))):
                bits = w_bits[:, 0:w.shape[1]]
                after(dve, s_wparts, 2 * n)
                link(coarse(bits, w), s_wbits, n + 1)
                nc.vector.tensor_copy(c, bits.bitcast(F32)).then_inc(s_wparts, 1)
                nc.vector.tensor_tensor(f, w, bits.bitcast(F32), ALU.subtract).then_inc(s_wparts, 1)
            dve.wait_ge(s_bdload, 48)
            split3(bdrow[:, :], bdrest[:, :], bdmid[:, :], bd3[:, :], s_bd, 0)
            attention_steps(dve, step)
            centre(2 * NQ - 1, NQ - 1)
            scale(2 * NQ - 1, NQ - 1)

            dve.wait_ge(s_rank, E)
            rk = rank[:, :].unsqueeze(1).to_broadcast([P, 3, E])
            bgv = bg_sb[:, :].unsqueeze(1).to_broadcast([P, 3, E])

            def wide(v):
                return v.unsqueeze(2).to_broadcast([P, 3, E])

            def fstep(k, s, h):
                n = k + 1
                dve.wait_ge(s_lg, n)
                link(nc.vector.tensor_tensor(lg[:, :, :], psL[s].rearrange("p (j e) -> p j e", e=E), bgv, ALU.add), s_lgb, n)
                link(nc.vector.tensor_reduce(lmax[:, :], lg[:, :, :], AX.X, ALU.max), s_lmax, n)
                link(nc.vector.tensor_tensor(ld[:, :, :], lg[:, :, :], wide(lmax[:, :]), ALU.subtract), s_lsub, n)
                link(nc.vector.scalar_tensor_tensor(out=lscore[:, :, :], in0=ld[:, :, :], scalar=0.0, in1=rk,
                                                    op0=ALU.is_equal, op1=ALU.mult), s_lscore, n)
                link(nc.vector.tensor_reduce(lbest[:, :], lscore[:, :, :], AX.X, ALU.max), s_lbest, n)
                nc.vector.tensor_tensor(lmask[:, :, :], lscore[:, :, :], wide(lbest[:, :]), ALU.is_equal).then_inc(s_lmask, 1)
                dve.wait_ge(s_gexp, n)
                link(nc.vector.tensor_reduce(lsum[:, :], le[:, :, :], AX.X, ALU.add), s_lsum, n)
                link(nc.vector.reciprocal(lrec[:, :], lsum[:, :]), s_lrec, n)
                dve.wait_ge(s_lmask, n)
                link(nc.vector.tensor_tensor(gate[:, :, :], lmask[:, :, :], wide(lrec[:, :]), ALU.mult), s_gate, n)
                for j in range(3):
                    dve.wait_ge(s_y, k * 3 + (j + 1))
                    link(nc.vector.tensor_tensor(z[:, j % 2, :, :], psY[j].rearrange("p (e c) -> p e c", e=E),
                                                 gate[:, j, :].unsqueeze(2).to_broadcast([P, E, F]), ALU.mult),
                         s_z, k * 3 + (j + 1))
                    nc.vector.tensor_reduce(ysel[:, j, :], z[:, j % 2, :, :].rearrange("p e c -> p c e"), AX.X,
                                            ALU.add).then_inc(s_ys, 1)
                dve.wait_ge(s_ys, k * 3 + 3)
                after(dve, s_out[s], h * 32)
                nc.vector.tensor_tensor(osb[s][:, :, :], ysel[:, :, :], psR[s].rearrange("p (j c) -> p j c", j=3),
                                        ALU.add).then_inc(s_fin, 1)

            steps(dve, 0, NF - 1, 2, NF - 1, fstep)

        @block.tensor
        def _(pe):
            mm = nc.tensor.matmul
            def score(q, lo, hi):
                for i in range(lo, hi):
                    pair = q * QP + i
                    if pair % (NPAIR // NX) == 0:
                        pe.wait_ge(s_x[pair // (NPAIR // NX)], 16)
                    last = mm(psScore[q], wscore[:, i * 96:i * 96 + 96], x_sb[:, pair, :], start=(i == 0), stop=(i == QP - 1))
                if hi == QP:
                    last.then_inc(s_score, 1)

            def broadcast(n, q, r):
                pe.wait_ge(s_wpc, q * 5 + 5)
                after(pe, s_wcp, n)
                after(pe, s_ln, q)
                if isinstance(n, int):
                    after(pe, s_prod, min(n, NR))
                for j in range(2):
                    last = mm(psW[:, j, :], sel[:, 2 * r + j, :], wpieces[:, :], start=True, stop=True)
                last.then_inc(s_wbc, 1)

            def mean(n, q):
                if n is q:
                    pe.wait_ge(s_pool, q * NR + NR)
                    pe.wait_ge(s_wcp, q * NR + NR)
                else:
                    pe.wait_ge(s_res, (q + 1) * QS)
                    pe.wait_ge(s_ln, n)
                mm(psLN, mean64[:, :], hT[:, at(q * QP, QP), :].rearrange("p r t -> p (r t)"),
                   start=True, stop=True).then_inc(s_mean, 1)

            def variance(n):
                pe.wait_ge(s_sq, n + 1)
                mm(psLN, mean64[:, :], sq[:, :], start=True, stop=True).then_inc(s_var, 1)

            def make_g(k, s):
                pe.wait_ge(s_xg[s], (k - s) * 32 + 64)
                after(pe, s_gev, k * 2)
                after(pe, s_pt, k - 2)
                for c in range(HC):
                    for i, w in enumerate((mm_coarse, mm_fine)):
                        last = mm(psG[:, c // 2, (c % 2) * G4:(c % 2 + 1) * G4], w[:, c * P:(c + 1) * P], XG[s][:, :, :],
                                  start=(i == 0), stop=(i == 1))
                    if c % 2 == 1:
                        last.then_inc(s_g, 1)

            def scores(k, s):
                pe.wait_ge(s_gev, k * 2 + 2)
                pe.wait_ge(s_xt[s], (k - s) * 32 + 64)
                if isinstance(k, int) and k == 0:
                    pe.wait_ge(s_wsub, NQ)
                after(pe, s_sub, k)
                after(pe, s_xb, k * 2)
                after(pe, s_res, k - 2)
                for b in range(4):
                    last = mm(psS[:, b // 2, (b % 2) * G4:(b % 2 + 1) * G4], XT[s][:, b, :],
                              G[s][:, :, b * NW:(b + 1) * NW], start=True, stop=True)
                last.then_inc(s_s, 1)

            def transpose_x(k, s):
                after(pe, s_cev, k - 1)
                for b in range(4):
                    bk = psS if b < 2 else psC
                    last = nc.tensor.transpose(bk[:, b % 2, 384:512], XT[s][:, b, :], ident[:, :])
                last.then_inc(s_xtr, 1)

            def transpose_p(k, s):
                pe.wait_ge(s_pn, k + 1)
                after(pe, s_pt, k)
                for b in range(4):
                    if b % 2 == 0:
                        pe.wait_ge(s_gev, k * 2 + (5 + b // 2) if runs(k + 2) else 2 * NSTEP)
                    for cc in range(2):
                        g = (b % 2) * 2 + cc
                        last = nc.tensor.transpose(psT[:, b // 2, g * P:(g + 1) * P],
                                                   Pn[s][:, b * 4 + 2 * cc:b * 4 + 2 * cc + 2, :].rearrange("p c u -> p (c u)"),
                                                   ident[:, :])
                last.then_inc(s_t, 1)

            def context(k, s):
                pe.wait_ge(s_pt, k + 1)
                pe.wait_ge(s_xb, k * 2 + (4 if runs(k + 1) else 2))
                after(pe, s_cev, k)
                for b in range(4):
                    last = mm(psC[:, b // 2, (b % 2) * G4:(b % 2 + 1) * G4], XB[s][:, b, :], PT[:, b, :],
                              start=True, stop=True)
                last.then_inc(s_c, 1)

            def project(k):
                pe.wait_ge(s_cev, k + 1)
                after(pe, s_res, k)
                pe.wait_ge(s_xb, k * 2 + 5 if runs(k + 2) else 2 * NSTEP)
                for b2 in range(2):
                    for g in range(4):
                        last = mm(psO[b2 * F:b2 * F + F, :], VOg[:, g, :], C[:, :, g, :].rearrange("p (r b) t -> p r b t", b=2)[:, :, b2, :],
                                  start=(g == 0), stop=(g == 3))
                last.then_inc(s_o, 1)

            def step(k, s, q=None, slot=None):
                if runs(k + 1):
                    scores(k + 1, 1 - s)
                if runs(k + 1):
                    transpose_x(k + 1, 1 - s)
                if runs(k + 2):
                    make_g(k + 2, s)
                if slot == 1 or slot == 2:
                    broadcast(q * NR + 2 * (slot - 1), q, 2 * (slot - 1))
                if runs(k):
                    transpose_p(k, s)
                if runs(k - 1):
                    project(k - 1)
                if slot == 3 or slot == 4:
                    mean(q + NQ if slot == 4 else q, q)
                if runs(k):
                    context(k, s)
                if slot == 3 or slot == 4:
                    variance(q + NQ if slot == 4 else q)
                if slot == 1 or slot == 2:
                    broadcast(q * NR + 2 * (slot - 1) + 1, q, 2 * (slot - 1) + 1)

            pe.wait_ge(s_wsc, 5)
            score(0, 0, QP)
            score(1, 0, QP)
            pe.wait_ge(s_aload, ALOADS)
            for h in range(H):
                last = mm(psMM[:, h * F:(h + 1) * F], k_sb[:, h, :, :].rearrange("r b d -> r (b d)"), q_sb[:, h, :], start=True, stop=True)
            last.then_inc(s_mm, 1)
            pe.wait_ge(s_sel, 3)
            for r in range(NR):
                broadcast(r, 0, r)
                score(2, 2 * r, 2 * r + 2)
            pe.wait_ge(s_zero, 1)
            first = 0
            mean(first, first)
            score(3, 0, 4)
            variance(0)
            score(3, 4, QP)
            pe.wait_ge(s_mmc, 2)
            pe.wait_ge(s_wsub, 2)
            pe.wait_ge(s_idt, 1)
            attention_steps(pe, step)
            mean(2 * NQ - 1, NQ - 1)
            variance(2 * NQ - 1)

            pe.wait_ge(s_wparts, 4)
            pe.wait_ge(s_bd, 5)

            def hidden(k, s, h):
                pe.wait_ge(s_xq[s], h * 96 + 96)
                after(pe, s_gelu, k * 2)
                for c in range(HCH):
                    for i, w in enumerate((w1_coarse, w1_fine)):
                        last = mm(psH[c], w[:, c * P:(c + 1) * P], xq[s][:, :], start=(i == 0), stop=(i == 1))
                last.then_inc(s_h, 1)

            def gates(k, s):
                pe.wait_ge(s_gelu, k * 2 + 2)
                after(pe, s_fin, k - 1)
                for j, t0 in enumerate(STARTS):
                    for c in range(HCH):
                        mm(psL[s][:, j * E:(j + 1) * E], Hs[s][:, c, t0:t0 + P], wg_sb[:, c, :],
                           start=(c == 0), stop=(c == HCH - 1))
                for j, t0 in enumerate(STARTS):
                    last = nc.tensor.transpose(psR[s][:, j * F:(j + 1) * F], hq[s][:, t0:t0 + P], ident[0:F, 0:F])
                last.then_inc(s_lg, 1)

            def experts(k, s):
                pe.wait_ge(s_hf, k + 1)
                for j, t0 in enumerate(STARTS):
                    after(pe, s_z, k * 3 + (j - 2))
                    for c in range(HCH):
                        for i, (h, w) in enumerate(((h_coarse, wd_coarse), (h_coarse, wd_fine), (h_fine, wd_coarse))):
                            mm(psY[j], h[s][:, c, t0:t0 + P], w[:, c, :], start=(c == 0 and i == 0), stop=False)
                    mm(psY[j], ones3[:, :], bd3[:, :], start=False, stop=True).then_inc(s_y, 1)

            def fstep(k, s, h):
                gates(k, s)
                if runs(k + 1, NF):
                    hidden(k + 1, 1 - s, h + s)
                experts(k, s)

            hidden(0, 0, 0)
            steps(pe, 0, NF - 1, 1, NF - 2, fstep)


_INS = ['x','L0_tok_w','L0_tok_b','L0_attn_Q','L0_attn_K','L0_attn_VO','L0_ffn_W1','L0_ffn_b1','L0_ffn_Wg','L0_ffn_bg','L0_ffn_Wd','L0_ffn_bd']
_OUTS = [((64, 47, 64), 'float32')]


def kernel(**inputs):
    import numpy as _np
    import concourse.bacc as _bacc
    from concourse import mybir as _mybir
    from concourse.bass_utils import run_bass_kernel_spmd as _run

    nc = _bacc.Bacc("TRN2", target_bir_lowering=False, num_devices=1)
    arrays, args = {}, []
    for name in _INS:
        a = _np.ascontiguousarray(inputs[name])
        arrays[f"in_{name}_dram"] = a
        args.append(nc.dram_tensor(f"in_{name}_dram", a.shape, _mybir.dt.from_np(a.dtype), kind="ExternalInput").ap())
    for i, (shape, dtype) in enumerate(_OUTS):
        dt = _mybir.dt.from_np(_np.dtype(dtype))
        args.append(nc.dram_tensor(f"out_{i}_dram", shape, dt, kind="ExternalOutput").ap())
    audio_tower_kernel(nc, *args)
    r = _run(nc, [arrays], core_ids=[0])
    got = tuple(r.results[0][f"out_{i}_dram"] for i in range(len(_OUTS)))
    return got[0]
```

```python
from contextlib import ExitStack

import concourse.bass as bass
from concourse import mybir

F32 = mybir.dt.float32
F32R = mybir.dt.float32r
I32 = mybir.dt.int32
BF16 = mybir.dt.bfloat16
ALU = mybir.AluOpType
ACT = mybir.ActivationFunctionType
AX = mybir.AxisListType


def audio_tower_kernel(nc, x, tok_w, tok_b, Q, K, VO, W1, b1, Wg, bg, Wd, bd, out):
    B, F, T_RAW = x.shape
    WIN = 8
    NW = -(-T_RAW // WIN)
    T = NW * WIN
    H, R, _ = Q.shape
    HID = W1.shape[1]
    E = Wg.shape[1]
    NPAIR = B // 2
    P = 128
    TP = 64
    NQ = 4
    QP = NPAIR // NQ
    NR = QP // 2
    HC = H // 2
    LNW = QP * NW
    NSTEP = NPAIR // 2
    G4 = 4 * NW
    QS = NSTEP // NQ
    NF = 8
    FT = 8 * NW
    HCH = HID // P
    STARTS = [0, P, FT - P]
    SKIP = 2 * P - (FT - P)
    EC = E * F
    EPS = 1e-5
    WARM = 4
    COARSE = -(1 << 12)

    with ExitStack() as ctx:
        def sb(name, shape, dt=F32):
            return ctx.enter_context(nc.sbuf_tensor(name, shape, dt))

        def ps(name, shape):
            return ctx.enter_context(nc.psum_tensor(name, shape, F32))

        def sem(name):
            return ctx.enter_context(nc.semaphore(name))

        x_sb = sb("x_sb", [P, NPAIR, T])
        wcol = sb("wcol", [P, 1])
        eps = sb("eps", [P, 1])
        tokb = sb("tokb", [P, 1])
        wscore = sb("wscore", [P, QP * (96 + 2)])
        sel = sb("sel", [96, QP, P], BF16)
        ident = sb("ident", [P, P])
        mean64 = sb("mean64", [P, P])
        ones3 = sb("ones3", [96, P], BF16)
        wmax = sb("wmax", [96, NW])
        wmaxb = sb("wmaxb", [96, NW])
        wexp = sb("wexp", [96, NQ, T])
        wsum = sb("wsum", [96, NW])
        wrec = sb("wrec", [96, NQ, NW])
        wrest = sb("wrest", [96, T])
        wmid = sb("wmid", [96, T], BF16)
        wpieces = sb("wpieces", [96, NQ, T], BF16)
        wbc = sb("wbc", [P, 2, 2, T])
        prod = sb("prod", [P, 2, 2, T])
        hT = sb("hT", [P, NPAIR, NW])
        xnT = sb("xnT", [P, NPAIR, NW])
        xn_coarse = sb("xn_coarse", [P, NPAIR, NW])
        xn_fine = sb("xn_fine", [P, NPAIR, NW])
        cen = sb("cen", [P, LNW])
        sq = sb("sq", [P, LNW])
        rstd = sb("rstd", [P, LNW])
        q_sb = sb("q_sb", [R, H, F])
        k_sb = sb("k_sb", [R, H, 2, F])
        XG = [sb(f"XG{s}", [P, 4, NW], F32R) for s in range(2)]
        mm_coarse = sb("mm_coarse", [P, HC * P], F32R)
        mm_fine = sb("mm_fine", [P, HC * P], F32R)
        VOg = sb("VOg", [P, 4, F])
        XT = [sb(f"XT{s}", [P, 4, P]) for s in range(2)]
        XB = [sb(f"XB{s}", [P, 4, P]) for s in range(2)]
        G = [sb(f"G{s}", [P, HC, G4]) for s in range(2)]
        rmax = sb("rmax", [P, 16])
        D = sb("D", [P, 16, NW])
        Ex = sb("Ex", [P, 16, NW])
        rsum = sb("rsum", [P, 16])
        rrec = [sb(f"rrec{s}", [P, 16]) for s in range(2)]
        Pn = [sb(f"Pn{s}", [P, 16, TP]) for s in range(2)]
        PT = sb("PT", [P, 4, G4])
        C = sb("C", [P, 4, 4, NW])
        w1_sb = sb("w1_sb", [P, HID])
        w1_coarse = sb("w1_coarse", [P, HID], F32R)
        w1_fine = sb("w1_fine", [P, HID], F32R)
        b1_sb = sb("b1_sb", [P, HCH])
        wg_sb = sb("wg_sb", [P, HCH, E])
        bg_sb = sb("bg_sb", [P, E])
        wd_sb = sb("wd_sb", [P, HCH, E, F])
        w_bits = sb("w_bits", [P, HCH * EC], I32)
        w1_bits = sb("w1_bits", [P, HID], I32)
        wd_coarse = sb("wd_coarse", [P, HCH, EC], F32R)
        wd_fine = sb("wd_fine", [P, HCH, EC], F32R)
        bdrow = sb("bdrow", [96, EC])
        bdmid = sb("bdmid", [96, EC], BF16)
        bd3 = sb("bd3", [96, EC], BF16)
        rank = sb("rank", [P, E])
        hq = [sb(f"hq{s}", [F, FT]) for s in range(2)]
        xq = [sb(f"xq{s}", [P, FT], F32R) for s in range(2)]
        Hs = [sb(f"Hs{s}", [P, HCH, FT]) for s in range(2)]
        h_coarse = [sb(f"h_coarse{s}", [P, HCH, FT], F32R) for s in range(2)]
        h_fine = [sb(f"h_fine{s}", [P, HCH, FT], F32R) for s in range(2)]
        lg = sb("lg", [P, 3, E])
        lmax = sb("lmax", [P, 3])
        ld = sb("ld", [P, 3, E])
        le = sb("le", [P, 3, E])
        lsum = sb("lsum", [P, 3])
        lrec = sb("lrec", [P, 3])
        lscore = sb("lscore", [P, 3, E])
        lbest = sb("lbest", [P, 3])
        lmask = sb("lmask", [P, 3, E])
        gate = sb("gate", [P, 3, E])
        z = x_sb[:, :, :].rearrange("p n t -> p (n t)")[:, 0:2 * EC].rearrange("p (s e f) -> p s e f", s=2, e=E)
        ysel = sb("ysel", [P, 3, F])
        osb = [sb(f"osb{s}", [P, 3, F]) for s in range(2)]

        bank = ps("bank", [P, 8, 512])

        psScore = [bank[0:96, i, 0:T] for i in range(NQ)]
        psMM = bank[:, 4, :]
        psW = bank[:, 6:8, 0:T]
        psLN = bank[:, 7, 0:LNW]
        psG = bank[:, 0:2, :]
        psT = bank[:, 0:2, :]
        psS = bank[:, 2:4, :]
        psO = bank[:, 2, 0:2 * NW]
        psC = bank[:, 4:6, :]
        psH = [bank[:, i, 0:FT] for i in (3, 6)]
        psL = [bank[:, i, 0:3 * E] for i in (0, 2)]
        psR = [bank[:, i, 64:64 + 3 * F] for i in (0, 2)]
        psY = [bank[:, i, :] for i in (4, 5, 1)]

        NX = 8
        s_x = [sem(f"s_x{i}") for i in range(NX)]
        s_wload = sem("s_wload")
        s_aload = sem("s_aload")
        s_fload = sem("s_fload")
        s_bdload = sem("s_bdload")
        ALOADS = 16 * (3 + 4)
        FLOADS = 16 * (5 + HCH)
        s_zero = sem("s_zero")
        s_vz = sem("s_vz")
        s_pz = sem("s_pz")
        s_sel = sem("s_sel")
        s_idt = sem("s_idt")
        s_wsc = sem("s_wsc")
        s_rank = sem("s_rank")
        s_warm = sem("s_warm")
        s_score = sem("s_score")
        s_wmax, s_wmaxb, s_wsub, s_wexp, s_wsum, s_wrec, s_wprob = [
            sem(n) for n in ("s_wmax", "s_wmaxb", "s_wsub", "s_wexp", "s_wsum", "s_wrec", "s_wprob")]
        s_wpc = sem("s_wpc")
        s_wbc = sem("s_wbc")
        s_wcp = sem("s_wcp")
        s_prod = sem("s_prod")
        s_prodp = sem("s_prodp")
        s_pool = sem("s_pool")
        s_mm = sem("s_mm")
        s_mmc = sem("s_mmc")
        s_mmb = sem("s_mmb")
        s_wbits = sem("s_wbits")
        s_wcoarse = sem("s_wcoarse")
        s_wfine = sem("s_wfine")
        s_mean = sem("s_mean")
        s_cen = sem("s_cen")
        s_sq = sem("s_sq")
        s_var = sem("s_var")
        s_ln = sem("s_ln")
        s_rstd = sem("s_rstd")
        s_nrm = sem("s_nrm")
        s_crs = sem("s_crs")
        s_xn = sem("s_xn")
        s_xt = [sem(f"s_xt{i}") for i in range(2)]
        s_xg = [sem(f"s_xg{i}") for i in range(2)]
        s_g = sem("s_g")
        s_gev = sem("s_gev")
        s_s = sem("s_s")
        s_xtr = sem("s_xtr")
        s_xb = sem("s_xb")
        s_max = sem("s_max")
        s_sub = sem("s_sub")
        s_exp = sem("s_exp")
        s_sum = sem("s_sum")
        s_rec = sem("s_rec")
        s_pn = sem("s_pn")
        s_t0 = sem("s_t0")
        s_t = sem("s_t")
        s_pt0 = sem("s_pt0")
        s_pt = sem("s_pt")
        s_c = sem("s_c")
        s_cev = sem("s_cev")
        s_o = sem("s_o")
        s_res = sem("s_res")
        s_bd = sem("s_bd")
        s_xq = [sem(f"s_xq{i}") for i in range(2)]
        s_h = sem("s_h")
        s_gelu = sem("s_gelu")
        s_hc = sem("s_hc")
        s_hf = sem("s_hf")
        s_lg = sem("s_lg")
        s_y = sem("s_y")
        s_lgb, s_lmax, s_lsub, s_gexp, s_lsum, s_lrec, s_lscore, s_lbest, s_lmask, s_gate = [
            sem(n) for n in ("s_lgb", "s_lmax", "s_lsub", "s_gexp", "s_lsum", "s_lrec", "s_lscore", "s_lbest",
                             "s_lmask", "s_gate")]
        s_z = sem("s_z")
        s_ys = sem("s_ys")
        s_fin = sem("s_fin")
        s_last = sem("s_last")
        s_out = [sem(f"s_out{i}") for i in range(2)]

        def after(eng, s, v):
            if not isinstance(v, int) or v > 0:
                eng.wait_ge(s, v)

        def steps(eng, first, last, lo, hi, body):
            for k in range(first, lo):
                body(k, k % 2, k // 2)
            if hi > lo:
                assert (hi + 1 - lo) % 2 == 0
                with eng.Fori(0, (hi + 1 - lo) // 2) as i:
                    for s in range(lo, lo + 2):
                        body(i * 2 + s, s % 2, i + s // 2)
            for k in range(max(hi, lo - 1) + 1, last + 1):
                body(k, k % 2, k // 2)

        def attention_steps(eng, step):
            step(-2, 0, 1, "round c")
            step(-1, 1, 1, "round d")
            step(0, 0, 1, "ln")
            with eng.Fori(2, NQ) as q:
                for j, work in enumerate(("rounds a", "rounds b", "ln begin", "ln end")):
                    step(q * QS + (j + 1 - 2 * QS), (j + 1) % 2, q, work)
            for k in range(2 * QS + 1, NSTEP + 1):
                step(k, k % 2, SECOND_LN.get(k), "ln2" if k in SECOND_LN else None)

        def link(eng, ins, s, n):
            ins.then_inc(s, 1)
            eng.wait_ge(s, n)

        def split3(eng, src, rest, mid, pieces, s, n):
            link(eng, eng.tensor_copy(pieces, src), s, n + 1)
            link(eng, eng.tensor_tensor(rest, src, pieces, ALU.subtract), s, n + 2)
            link(eng, eng.tensor_copy(mid, rest), s, n + 3)
            link(eng, eng.tensor_copy(pieces[32:64], mid[32:64]), s, n + 4)
            link(eng, eng.tensor_tensor(pieces[64:96], rest[64:96], mid[64:96], ALU.subtract), s, n + 5)

        TWO_ROUNDS = {"rounds a": 0, "rounds b": 2}
        ONE_ROUND = {"round c": 2, "round d": 3}
        SECOND_LN = {9: 0, 11: 1, 13: 2}
        LN_ENDS = {k + 1: (NQ + q, q) for k, q in SECOND_LN.items()}
        BIAS_STEPS = [9, 10, 11, 12, 13]
        BITS_STEP, COARSE_STEP, FINE_STEP = 9, 10, 11

        def ln_end(k, q, work):
            return (q, q) if work in ("ln", "ln end") else LN_ENDS.get(k) if isinstance(k, int) else None

        def runs(k, n=NSTEP):
            return not isinstance(k, int) or 0 <= k < n

        def at(k, n):
            return slice(k, k + n) if isinstance(k, int) else bass.ds(k, n)

        block = ctx.enter_context(nc.Block())

        @block.sync
        def _(sp):
            xv = x.rearrange("(p b) f t -> (b f) p t", b=2)
            per = NPAIR // NX
            for b2 in range(2):
                sp.dma_start(wcol[b2 * F:b2 * F + F, :], tok_w.rearrange("o f -> f o")).then_inc(s_wload, 16)
            for i in range(NX):
                sp.dma_start(x_sb[:, i * per:(i + 1) * per, 0:T_RAW], xv[:, i * per:(i + 1) * per, :]).then_inc(s_x[i], 16)

            for half in range(2):
                sp.dma_start(w1_sb[half * F:half * F + F, :], W1).then_inc(s_fload, 16)
            sp.dma_start(b1_sb[:, :], b1.rearrange("(c p) -> p c", p=P), allow_slow_non_contiguous=True).then_inc(s_fload, 16)
            sp.dma_start(wg_sb[:, :, :], Wg.rearrange("(c p) e -> p c e", p=P)).then_inc(s_fload, 16)
            sp.dma_start(bg_sb[:, :], bg.rearrange("(o e) -> o e", o=1).to_broadcast([P, E])).then_inc(s_fload, 16)
            for c in range(HCH):
                sp.dma_start(wd_sb[:, c, :, :], Wd[:, c * P:(c + 1) * P, :].rearrange("e p c -> p e c")).then_inc(s_fload, 16)
            sp.wait_ge(s_vz, 4)
            for j in range(3):
                sp.dma_start(bdrow[32 * j:32 * j + 1, :], bd.rearrange("(o e) c -> o (e c)", o=1)).then_inc(s_bdload, 16)

            def load_x(k, s):
                after(sp, s_xtr, k - 1)
                for half, src in enumerate((xn_coarse, xn_fine)):
                    dst = XG[s][half * F:half * F + F, :, :].bitcast(F32).rearrange("p (r b) t -> p r b t", b=2)
                    for b2 in range(2):
                        sp.dma_start(dst[:, :, b2, :], src[b2 * F:b2 * F + F, at(k * 2, 2), :]).then_inc(s_xg[s], 16)
                dst = XT[s][:, :, :].rearrange("p (r b) c -> p r b c", b=2)
                for b2 in range(2):
                    for par in range(2):
                        sp.dma_start(dst[par * TP:par * TP + F, :, b2, par * TP:par * TP + NW],
                                     xnT[b2 * F:b2 * F + F, at(k * 2, 2), :]).then_inc(s_xt[s], 16)

            sp.wait_ge(s_zero, 1)
            sp.wait_ge(s_xn, 1)
            for k in range(QS):
                load_x(k, k % 2)
            with sp.Fori(1, NQ) as q:
                sp.wait_ge(s_xn, q + 1)
                for j in range(QS):
                    load_x(q * QS + j, j % 2)

            def load_xq(k, s, h):
                sp.wait_ge(s_xn, h + (NQ + 1))
                after(sp, s_lg, k - 1)
                for to, src in ((xq[s][0:F, :].bitcast(F32), xn_coarse), (xq[s][F:P, :].bitcast(F32), xn_fine),
                                (hq[s][:, :], hT)):
                    dst = to.rearrange("p (r b t) -> p r b t", b=2, t=NW)
                    for b2 in range(2):
                        sp.dma_start(dst[:, :, b2, :], src[b2 * F:b2 * F + F, at(k * 4, 4), :]).then_inc(s_xq[s], 16)

            steps(sp, 0, NF - 1, 2, NF - 1, load_xq)

            sp.wait_ge(s_fin, NF)
            o = out.rearrange("b t c -> (b t) c")[(NF - 1) * FT:NF * FT, :]
            sp.dma_start(o[0:2 * P, :].rearrange("(j p) c -> p j c", p=P), osb[1][:, 0:2, :]).then_inc(s_last, 16)
            sp.dma_start(o[2 * P:FT, :], osb[1][SKIP:P, 2, :]).then_inc(s_last, 16)
            sp.wait_ge(s_last, 32)

        @block.gpsimd
        def _(pool):
            pool.memset(ident[:, :], 0.0).then_inc(s_pz, 1)
            pool.memset(sel[:, :, :], 0.0).then_inc(s_pz, 1)
            pool.wait_ge(s_pz, 2)
            pool.affine_select(out=ident[:, :], in_=ident[:, :], compare_op=ALU.not_equal, fill=1.0,
                               base=0, pattern=[[-1, P]], channel_multiplier=1).then_inc(s_idt, 1)
            for j in range(3):
                pool.wait_ge(s_idt if j == 0 else s_sel, max(j, 1))
                v = sel[32 * j:32 * j + 32, :, :].rearrange("q i (b f) -> q i b f", b=2)
                pool.affine_select(out=v, in_=v, compare_op=ALU.not_equal, fill=1.0, base=0,
                                   pattern=[[-2, QP], [-1, 2], [0, F]], channel_multiplier=1).then_inc(s_sel, 1)
            pool.wait_ge(s_sel, 3)
            for s in range(2):
                pool.memset(Pn[s][:, :, :], 0.0).then_inc(s_pz, 1)
            pool.wait_ge(s_pz, 4)
            for e in range(E):
                pool.memset(rank[:, e:e + 1], float(E - e)).then_inc(s_rank, 1)

            def round_products(n, s, direct=0):
                pool.wait_ge(s_wcp, n + 1)
                after(pool, s_pool, n - 1)
                pool.tensor_tensor(prod[:, s, direct:2, :], x_sb[:, at(n * 2 + direct, 2 - direct), :],
                                   wbc[:, s, direct:2, :], ALU.mult).then_inc(s_prodp, 1)

            def normalise(k, s):
                pool.wait_ge(s_rec, k + 1)
                after(pool, s_t, k - 1)
                pool.tensor_tensor(Pn[s][:, :, 0:NW], Ex[:, :, :],
                                   rrec[s][:, :].unsqueeze(2).to_broadcast([P, 16, NW]),
                                   ALU.mult).then_inc(s_pn, 1)

            def window_weights(q):
                pool.wait_ge(s_wprob, q + 1)
                split3(pool, wexp[:, q, :], wrest[:, :], wmid[:, :], wpieces[:, q, :], s_wpc, q * 5)

            def step(k, s, q=None, work=None):
                if work in TWO_ROUNDS:
                    round_products(q * NR + TWO_ROUNDS[work], 0)
                if runs(k + 1):
                    normalise(k + 1, 1 - s)
                if work in TWO_ROUNDS:
                    round_products(q * NR + (TWO_ROUNDS[work] + 1), 1)
                if work in ONE_ROUND:
                    round_products(q * NR + ONE_ROUND[work], ONE_ROUND[work] % 2)
                if work == "round c":
                    pool.wait_ge(s_prodp, NR + 3)
                    window_weights(2)
                if work == "ln":
                    pool.wait_ge(s_pn, 2)
                    window_weights(3)
                if isinstance(k, int) and k in BIAS_STEPS:
                    split_bias(k, BIAS_STEPS.index(k))
                if isinstance(k, int) and k == FINE_STEP:
                    fine_weights()

            def fine_weights():
                pool.wait_ge(s_wbits, 2)
                for f, w, bits in ((w1_fine[:, :], w1_sb[:, :], w1_bits),
                                   (wd_fine[:, :, :].rearrange("p c m -> p (c m)"),
                                    wd_sb[:, :, :, :].rearrange("p c e f -> p (c e f)"), w_bits)):
                    pool.tensor_tensor(f, w, bits[:, :].bitcast(F32), ALU.subtract).then_inc(s_wfine, 1)

            def split_bias(k, i):
                rest = z[0:96, 0, :, :].rearrange("p e c -> p (e c)")
                pool.wait_ge(s_bdload, 48)
                after(pool, s_bd, i)
                pool.wait_ge(s_pn, k + 2)
                if i == 0:
                    ins = pool.tensor_copy(bd3[:, :], bdrow[:, :])
                elif i == 1:
                    ins = pool.tensor_tensor(rest, bdrow[:, :], bd3[:, :], ALU.subtract)
                elif i == 2:
                    ins = pool.tensor_copy(bdmid[:, :], rest)
                elif i == 3:
                    ins = pool.tensor_copy(bd3[32:64], bdmid[32:64])
                else:
                    ins = pool.tensor_tensor(bd3[64:96], rest[64:96], bdmid[64:96], ALU.subtract)
                link(pool, ins, s_bd, i + 1)

            for n in range(NR):
                round_products(n, n % 2, direct=1)
            for n in range(2):
                round_products(NR + n, n)
            attention_steps(pool, step)

            def fine_hidden(k, s):
                pool.wait_ge(s_hc, k + 1)
                after(pool, s_y, 3 * (k - 1))
                pool.tensor_tensor(h_fine[s][:, :, :], Hs[s][:, :, :], h_coarse[s][:, :, :], ALU.subtract).then_inc(s_hf, 1)

            def store(k, s, _):
                if runs(k + 1, NF):
                    fine_hidden(k + 1, 1 - s)
                pool.wait_ge(s_fin, k + 1)
                o = out.rearrange("b t c -> (b t) c")[at(k * FT, FT), :]
                pool.dma_start(o[0:2 * P, :].rearrange("(j p) c -> p j c", p=P), osb[s][:, 0:2, :]).then_inc(s_out[s], 16)
                pool.dma_start(o[2 * P:FT, :], osb[s][SKIP:P, 2, :]).then_inc(s_out[s], 16)

            fine_hidden(0, 0)
            steps(pool, 0, NF - 2, 1, NF - 2, store)
            for s in range(2):
                pool.wait_ge(s_out[s], 32 * (NF // 2 - s))

        @block.scalar
        def _(act):
            act.preload_act_table_set("natural_log_exp_and_others")
            act.dma_start(tokb[:, :], tok_b.rearrange("(o a) -> o a", a=1).to_broadcast([P, 1])).then_inc(s_wload, 16)
            act.dma_start(q_sb[:, :, :], Q.rearrange("h r d -> r h d")).then_inc(s_aload, 16)
            for copy in range(2):
                act.dma_start(k_sb[:, :, copy, :], K.rearrange("h r d -> r h d")).then_inc(s_aload, 16)
            vov = VO.rearrange("(cc c2 par) d e -> c2 d cc par e", c2=2, par=2)
            for c2 in range(2):
                for cc in range(2):
                    act.dma_start(VOg[c2 * F:c2 * F + F, 2 * cc:2 * cc + 2, :], vov[c2, :, cc]).then_inc(s_aload, 16)
            def window_exp(q):
                act.wait_ge(s_wsub, q + 1)
                nc.scalar.activation(wexp[:, q, :], wexp[:, q, :], ACT.Exp).then_inc(s_wexp, 1)

            def copy_weights(n, s, direct=0):
                act.wait_ge(s_wbc, n + 1)
                after(act, s_prodp, n - 1)
                nc.scalar.copy(wbc[:, s, direct:2, :], psW[:, direct:2, :]).then_inc(s_wcp, 1)

            def square(n):
                act.wait_ge(s_cen, n + 1)
                nc.scalar.activation(sq[:, :], cen[:, :], ACT.Square).then_inc(s_sq, 1)

            def inverse_root(n):
                act.wait_ge(s_var, n + 1)
                nc.scalar.activation(sq[:, :], psLN, ACT.Ln, bias=eps[:, 0:1]).then_inc(s_ln, 1)
                act.wait_ge(s_ln, n + 1)
                nc.scalar.activation(rstd[:, :], sq[:, :], ACT.Exp, scale=-0.5).then_inc(s_rstd, 1)

            def evac_g(k, s):
                after(act, s_s, k * 2 - 2)
                for a in range(2):
                    act.wait_ge(s_g, k * 2 + (a + 1))
                    nc.scalar.copy(G[s][:, 2 * a:2 * a + 2, :].rearrange("p c n -> p (c n)"), psG[:, a, 0:2 * G4]).then_inc(s_gev, 1)

            def exp(k):
                act.wait_ge(s_sub, k * 2 + 2)
                after(act, s_pn, k)
                nc.scalar.activation(Ex[:, :, :], D[:, :, :], ACT.Exp, scale=float(F) ** -0.5).then_inc(s_exp, 1)

            def evac_t(k):
                after(act, s_c, k)
                for a, (made, out_) in enumerate(((s_t0, s_pt0), (s_t, s_pt))):
                    act.wait_ge(made, k + 1)
                    nc.scalar.copy(PT[:, 2 * a:2 * a + 2, :].rearrange("p b (g t) -> p (b g) t", t=NW),
                                   psT[:, a, :].rearrange("p (g t) -> p g t", t=TP)[:, :, 0:NW]).then_inc(out_, 1)

            def evac_c(k):
                act.wait_ge(s_c, k + 1)
                after(act, s_o, k)
                nc.scalar.copy(C[:, :, :, :].rearrange("p (k b) g t -> p k b (g t)", k=2),
                               psC[:, :, 0:2 * G4].rearrange("p k (b n) -> p k b n", b=2)).then_inc(s_cev, 1)

            def gelu(k, s):
                act.wait_ge(s_h, k + 1)
                after(act, s_y, 3 * (k - 1))
                for c in range(HCH):
                    nc.scalar.activation(Hs[s][:, c, :], psH[c], ACT.Gelu, bias=b1_sb[:, c:c + 1]).then_inc(s_gelu, 1)

            def coarse_hidden(k, s):
                act.wait_ge(s_gelu, k * 2 + 2)
                after(act, s_y, 3 * (k - 1))
                nc.scalar.copy(h_coarse[s][:, :, :], Hs[s][:, :, :]).then_inc(s_hc, 1)

            def step(k, s, q=None, work=None):
                if isinstance(k, int) and k == NSTEP - 1:
                    act.wait_ge(s_fload, FLOADS)
                    act.preload_act_table_set("gelu_and_others")
                    gelu(0, 0)
                ln = q + NQ if work == "ln2" else q
                if runs(k + 2):
                    evac_g(k + 2, s)
                if ln_end(k, q, work) and work != "ln":
                    inverse_root(ln_end(k, q, work)[0])
                if runs(k):
                    evac_t(k)
                if runs(k + 1):
                    exp(k + 1)
                if work in TWO_ROUNDS:
                    copy_weights(q * NR + TWO_ROUNDS[work], 0)
                if isinstance(k, int) and k == NSTEP - 1:
                    coarse_hidden(0, 0)
                if runs(k):
                    evac_c(k)
                if work in ("ln", "ln begin", "ln2"):
                    square(ln)
                if work == "ln":
                    inverse_root(ln)
                if work in ONE_ROUND:
                    copy_weights(q * NR + ONE_ROUND[work], ONE_ROUND[work] % 2)
                if work == "round c":
                    window_exp(3)
                if work in TWO_ROUNDS:
                    copy_weights(q * NR + (TWO_ROUNDS[work] + 1), 1)
                if isinstance(k, int) and k == COARSE_STEP:
                    for n, (c, bits) in enumerate(((w1_coarse[:, :], w1_bits),
                                                   (wd_coarse[:, :, :].rearrange("p c m -> p (c m)"), w_bits))):
                        act.wait_ge(s_wbits, n + 1)
                        nc.scalar.copy(c, bits[:, :].bitcast(F32)).then_inc(s_wcoarse, 1)

            window_exp(0)
            for n in range(NR):
                copy_weights(n, n % 2, direct=1)
            window_exp(1)
            square(0)
            inverse_root(0)
            for n in range(2):
                copy_weights(NR + n, n)
            window_exp(2)
            attention_steps(act, step)

            def gate_exp(k):
                act.wait_ge(s_lsub, k + 1)
                nc.scalar.activation(le[:, :, :], ld[:, :, :], ACT.Exp).then_inc(s_gexp, 1)

            act.preload_act_table_set("natural_log_exp_and_others")
            gate_exp(0)
            act.preload_act_table_set("gelu_and_others")
            gelu(1, 1)
            coarse_hidden(1, 1)
            square(2 * NQ - 1)
            act.preload_act_table_set("natural_log_exp_and_others")
            inverse_root(2 * NQ - 1)

            def fstep(k, s, _):
                act.preload_act_table_set("exp_and_others")
                gate_exp(k)
                if runs(k + 1, NF):
                    act.preload_act_table_set("gelu_and_others")
                    gelu(k + 1, 1 - s)
                    coarse_hidden(k + 1, 1 - s)

            steps(act, 1, NF - 1, 1, NF - 2, fstep)

        @block.vector
        def _(dve):
            def coarse(bits, v):
                return nc.vector.tensor_scalar(bits, v.bitcast(I32), COARSE, None, ALU.bitwise_and)

            nc.vector.memset(prod[:, 0, 0, :], 0.0).then_inc(s_wsc, 1)
            nc.vector.memset(wscore[:, :], 0.0).then_inc(s_wsc, 1)
            nc.vector.memset(x_sb[:, :, T_RAW:T], 0.0).then_inc(s_wsc, 1)
            nc.vector.memset(eps[:, :], EPS).then_inc(s_wsc, 1)
            dve.wait_ge(s_wsc, 4)
            dve.wait_ge(s_wload, 48)
            for b2 in range(2):
                dst = wscore[b2 * F:b2 * F + F, :].rearrange("p (i c) -> p i c", c=98)[:, :, b2:b2 + 65:32]
                nc.vector.tensor_copy(dst, wcol[b2 * F:b2 * F + F, :].unsqueeze(2).to_broadcast([F, QP, 3])).then_inc(s_wsc, 1)
            for v in (XT[0][:, :, :], XT[1][:, :, :]):
                nc.vector.memset(v, 0.0).then_inc(s_vz, 1)
            nc.vector.memset(bdrow[:, :], 0.0).then_inc(s_vz, 1)
            nc.vector.memset(mean64[:, :], 0.0).then_inc(s_vz, 1)
            dve.wait_ge(s_vz, 4)
            for b2 in range(2):
                nc.vector.memset(mean64[b2 * F:b2 * F + F, b2 * F:b2 * F + F], 1.0 / F).then_inc(s_vz, 1)
            dve.wait_ge(s_vz, 6)
            nc.vector.memset(ones3[:, :], 1.0).then_inc(s_zero, 1)

            win = "p (w k) -> p w k"
            def window_max(q):
                n = q + 1
                dve.wait_ge(s_score, n)
                sq_ = psScore[q].rearrange(win, k=WIN)
                link(dve, nc.vector.tensor_reduce(wmax[:, :], sq_, AX.X, ALU.max), s_wmax, n)
                link(dve, nc.vector.tensor_scalar(wmaxb[:, :], wmax[:, :], tokb[0:96, 0:1], None, ALU.add), s_wmaxb, n)
                nc.vector.scalar_tensor_tensor(
                    out=wexp[:, q, :].rearrange(win, k=WIN), in0=sq_, scalar=tokb[0:96, 0:1],
                    in1=wmaxb[:, :].unsqueeze(2).to_broadcast([96, NW, WIN]), op0=ALU.add,
                    op1=ALU.subtract).then_inc(s_wsub, 1)

            def window_probs(q):
                n = q + 1
                dve.wait_ge(s_wexp, n)
                link(dve, nc.vector.tensor_reduce(wsum[:, :], wexp[:, q, :].rearrange(win, k=WIN), AX.X, ALU.add), s_wsum, n)
                link(dve, nc.vector.reciprocal(wrec[:, q, :], wsum[:, :]), s_wrec, n)
                link(dve, nc.vector.tensor_tensor(wexp[:, q, :].rearrange(win, k=WIN), wexp[:, q, :].rearrange(win, k=WIN),
                                                  wrec[:, q, :].unsqueeze(2).to_broadcast([96, NW, WIN]), ALU.mult), s_wprob, q + 1)

            def window_weights(q):
                split3(dve, wexp[:, q, :], wrest[:, :], wmid[:, :], wpieces[:, q, :], s_wpc, q * 5)

            def direct_product(n, s):
                dve.wait_ge(s_wbc, n + 1)
                after(dve, s_pool, n - 1)
                if n == 0:
                    dve.wait_ge(s_warm, WARM)
                nc.vector.tensor_tensor(prod[:, s, 0, :], x_sb[:, 2 * n, :], psW[:, 0, :], ALU.mult).then_inc(s_prod, 1)

            def pool_round(n, s):
                if isinstance(n, int) and n < NR:
                    dve.wait_ge(s_prod, n + 1)
                dve.wait_ge(s_prodp, n + 1)
                nc.vector.tensor_reduce(hT[:, at(n * 2, 2), :], prod[:, s, :, :].rearrange("p j (w k) -> p j w k", k=WIN),
                                        AX.X, ALU.add).then_inc(s_pool, 1)

            def quarter(t, q):
                return t[:, at(q * QP, QP), :].rearrange("p r t -> p (r t)")

            def centre(n, q):
                dve.wait_ge(s_mean, n + 1)
                nc.vector.tensor_tensor(cen[:, :], quarter(hT, q), psLN, ALU.subtract).then_inc(s_cen, 1)

            def scale(n, q):
                dve.wait_ge(s_rstd, n + 1)
                nc.vector.tensor_tensor(quarter(xnT, q), cen[:, :], rstd[:, :], ALU.mult).then_inc(s_nrm, 1)

            def split_xn(n, q):
                dve.wait_ge(s_nrm, n + 1)
                link(dve, coarse(quarter(xn_coarse, q).bitcast(I32), quarter(xnT, q)), s_crs, n + 1)
                nc.vector.tensor_tensor(quarter(xn_fine, q), quarter(xnT, q), quarter(xn_coarse, q), ALU.subtract).then_inc(s_xn, 1)

            sS = psS[:, :, 0:2 * G4].rearrange("p k (g u) -> p k g u", u=NW)

            def max_sub(k, s):
                for a in range(2):
                    dve.wait_ge(s_s, k * 2 + (a + 1))
                    nc.vector.tensor_reduce(rmax[:, 8 * a:8 * a + 8], sS[:, a], AX.X, ALU.max).then_inc(s_max, 1)
                    if a == 0:
                        after(dve, s_c, k - 1)
                    nc.vector.tensor_copy(XB[s][:, a, :], psS[:, a, 384:512]).then_inc(s_xb, 1)
                after(dve, s_exp, k)
                for a in range(2):
                    dve.wait_ge(s_max, k * 2 + (a + 1))
                    nc.vector.tensor_tensor(D[:, 8 * a:8 * a + 8, :], sS[:, a],
                                            rmax[:, 8 * a:8 * a + 8].unsqueeze(2).to_broadcast([P, 8, NW]),
                                            ALU.subtract).then_inc(s_sub, 1)
                dve.wait_ge(s_xtr, k + 1)
                nc.vector.tensor_copy(XB[s][:, 2:4, :], psC[:, :, 384:512]).then_inc(s_xb, 1)

            def row_sum(k, s):
                dve.wait_ge(s_exp, k + 1)
                link(dve, nc.vector.tensor_reduce(rsum[:, :], Ex[:, :, :], AX.X, ALU.add), s_sum, k + 1)
                after(dve, s_pn, k - 1)
                nc.vector.reciprocal(rrec[s][:, :], rsum[:, :]).then_inc(s_rec, 1)

            def residual(k):
                dve.wait_ge(s_o, k + 1)
                h = hT[:, at(k * 2, 2), :].rearrange("p r t -> p (r t)")
                nc.vector.tensor_tensor(h, h, psO, ALU.add).then_inc(s_res, 1)

            def step(k, s, q=None, work=None):
                ln = q + NQ if work == "ln2" else q
                if runs(k + 1):
                    max_sub(k + 1, 1 - s)
                if ln_end(k, q, work) and work != "ln" and runs(k + 2):
                    scale(*ln_end(k, q, work))
                if work in ("ln", "ln begin"):
                    pool_round(q * NR + 2, 0)
                    pool_round(q * NR + 3, 1)
                if work == "rounds b":
                    pool_round(q * NR, 0)
                if runs(k - 1) and not (isinstance(k, int) and k == NSTEP):
                    residual(k - 1)
                if runs(k + 1):
                    row_sum(k + 1, 1 - s)
                if ln_end(k, q, work) and work != "ln" and runs(k + 2):
                    split_xn(*ln_end(k, q, work))
                if work in ("ln", "ln begin", "ln2"):
                    centre(ln, q)
                if work == "rounds b":
                    pool_round(q * NR + 1, 1)
                if work == "ln":
                    window_probs(3)
                    scale(q, q)
                    split_xn(q, q)
                if ln_end(k, q, work) and not runs(k + 2):
                    scale(*ln_end(k, q, work))
                    split_xn(*ln_end(k, q, work))
                if isinstance(k, int) and k == BITS_STEP:
                    dve.wait_ge(s_mmc, 2)
                    dve.wait_ge(s_fload, FLOADS)
                    for bits, w in ((w1_bits, w1_sb[:, :]), (w_bits, wd_sb[:, :, :, :].rearrange("p c e f -> p (c e f)"))):
                        coarse(bits[:, :], w).then_inc(s_wbits, 1)

            window_max(0)
            window_probs(0)
            window_weights(0)
            direct_product(0, 0)
            direct_product(1, 1)
            pool_round(0, 0)
            direct_product(2, 0)
            pool_round(1, 1)
            direct_product(3, 1)
            pool_round(2, 0)
            pool_round(3, 1)
            window_max(1)
            centre(0, 0)
            window_probs(1)
            scale(0, 0)
            split_xn(0, 0)
            window_weights(1)
            dve.wait_ge(s_mm, 1)
            link(dve, coarse(w_bits[:, 0:HC * P], psMM), s_mmb, 1)
            nc.vector.tensor_copy(mm_coarse[:, :], w_bits[:, 0:HC * P].bitcast(F32)).then_inc(s_mmc, 1)
            nc.vector.tensor_tensor(mm_fine[:, :], psMM, w_bits[:, 0:HC * P].bitcast(F32), ALU.subtract).then_inc(s_mmc, 1)
            window_max(2)
            window_max(3)
            pool_round(NR, 0)
            window_probs(2)
            pool_round(NR + 1, 1)
            attention_steps(dve, step)

            dve.wait_ge(s_rank, E)
            rk = rank[:, :].unsqueeze(1).to_broadcast([P, 3, E])
            bgv = bg_sb[:, :].unsqueeze(1).to_broadcast([P, 3, E])

            def wide(v):
                return v.unsqueeze(2).to_broadcast([P, 3, E])

            def choose(k, s):
                n = k + 1
                dve.wait_ge(s_lg, n)
                link(dve, nc.vector.tensor_tensor(lg[:, :, :], psL[s].rearrange("p (j e) -> p j e", e=E), bgv, ALU.add), s_lgb, n)
                link(dve, nc.vector.tensor_reduce(lmax[:, :], lg[:, :, :], AX.X, ALU.max), s_lmax, n)
                link(dve, nc.vector.tensor_tensor(ld[:, :, :], lg[:, :, :], wide(lmax[:, :]), ALU.subtract), s_lsub, n)
                link(dve, nc.vector.scalar_tensor_tensor(out=lscore[:, :, :], in0=ld[:, :, :], scalar=0.0, in1=rk,
                                                    op0=ALU.is_equal, op1=ALU.mult), s_lscore, n)
                link(dve, nc.vector.tensor_reduce(lbest[:, :], lscore[:, :, :], AX.X, ALU.max), s_lbest, n)
                nc.vector.tensor_tensor(lmask[:, :, :], lscore[:, :, :], wide(lbest[:, :]), ALU.is_equal).then_inc(s_lmask, 1)

            def mix(k, s, h):
                n = k + 1
                dve.wait_ge(s_gexp, n)
                link(dve, nc.vector.tensor_reduce(lsum[:, :], le[:, :, :], AX.X, ALU.add), s_lsum, n)
                link(dve, nc.vector.reciprocal(lrec[:, :], lsum[:, :]), s_lrec, n)
                dve.wait_ge(s_lmask, n)
                link(dve, nc.vector.tensor_tensor(gate[:, :, :], lmask[:, :, :], wide(lrec[:, :]), ALU.mult), s_gate, n)
                for j in range(3):
                    dve.wait_ge(s_y, k * 3 + (j + 1))
                    link(dve, nc.vector.tensor_tensor(z[:, j % 2, :, :], psY[j].rearrange("p (e c) -> p e c", e=E),
                                                 gate[:, j, :].unsqueeze(2).to_broadcast([P, E, F]), ALU.mult),
                         s_z, k * 3 + (j + 1))
                    nc.vector.tensor_reduce(ysel[:, j, :], z[:, j % 2, :, :].rearrange("p e c -> p c e"), AX.X,
                                            ALU.add).then_inc(s_ys, 1)
                dve.wait_ge(s_ys, k * 3 + 3)
                after(dve, s_out[s], h * 32)
                nc.vector.tensor_tensor(osb[s][:, :, :], ysel[:, :, :], psR[s].rearrange("p (j c) -> p j c", j=3),
                                        ALU.add).then_inc(s_fin, 1)

            def fstep(k, s, h):
                choose(k, s)
                mix(k, s, h)

            choose(0, 0)
            residual(NSTEP - 1)
            centre(2 * NQ - 1, NQ - 1)
            mix(0, 0, 0)
            scale(2 * NQ - 1, NQ - 1)
            split_xn(2 * NQ - 1, NQ - 1)
            steps(dve, 1, NF - 1, 2, NF - 1, fstep)

        @block.tensor
        def _(pe):
            mm = nc.tensor.matmul
            def score(q, lo, hi):
                for i in range(lo, hi):
                    pair = q * QP + i
                    if pair % (NPAIR // NX) == 0:
                        pe.wait_ge(s_x[pair // (NPAIR // NX)], 16)
                    last = mm(psScore[q], wscore[:, i * 96:i * 96 + 96], x_sb[:, pair, :], start=(i == 0), stop=(i == QP - 1))
                if hi == QP:
                    last.then_inc(s_score, 1)

            def broadcast(n, q, r):
                pe.wait_ge(s_wpc, q * 5 + 5)
                after(pe, s_wcp, n)
                after(pe, s_ln, q)
                if isinstance(n, int):
                    after(pe, s_prod, min(n, NR))
                for j in range(2):
                    last = mm(psW[:, j, :], sel[:, 2 * r + j, :], wpieces[:, at(q, 1), :], start=True, stop=True)
                last.then_inc(s_wbc, 1)

            def mean(n, q, second=False):
                if not second:
                    pe.wait_ge(s_pool, q * NR + NR)
                    pe.wait_ge(s_wcp, q * NR + NR)
                else:
                    pe.wait_ge(s_res, (q + 1) * QS)
                    pe.wait_ge(s_ln, n)
                mm(psLN, mean64[:, :], hT[:, at(q * QP, QP), :].rearrange("p r t -> p (r t)"),
                   start=True, stop=True).then_inc(s_mean, 1)

            def variance(n):
                pe.wait_ge(s_sq, n + 1)
                mm(psLN, mean64[:, :], sq[:, :], start=True, stop=True).then_inc(s_var, 1)

            def make_g(k, s):
                pe.wait_ge(s_xg[s], (k - s) * 32 + 64)
                after(pe, s_gev, k * 2)
                after(pe, s_pt, k - 2)
                for c in range(HC):
                    for i, w in enumerate((mm_coarse, mm_fine)):
                        last = mm(psG[:, c // 2, (c % 2) * G4:(c % 2 + 1) * G4], w[:, c * P:(c + 1) * P], XG[s][:, :, :],
                                  start=(i == 0), stop=(i == 1))
                    if c % 2 == 1:
                        last.then_inc(s_g, 1)

            def scores(k, s):
                pe.wait_ge(s_gev, k * 2 + 2)
                pe.wait_ge(s_xt[s], (k - s) * 32 + 64)
                if isinstance(k, int) and k == 0:
                    pe.wait_ge(s_wsub, NQ)
                after(pe, s_sub, k * 2)
                after(pe, s_xb, k * 3)
                after(pe, s_res, k - 2)
                for b in range(4):
                    mm(psS[:, b // 2, (b % 2) * G4:(b % 2 + 1) * G4], XT[s][:, b, :],
                       G[s][:, :, b * NW:(b + 1) * NW], start=True, stop=True)
                    if b % 2 == 1:
                        nc.tensor.transpose(psS[:, b // 2, 384:512], XT[s][:, b // 2, :], ident[:, :]).then_inc(s_s, 1)

            def transpose_x(k, s):
                after(pe, s_cev, k - 1)
                for b in (2, 3):
                    last = nc.tensor.transpose(psC[:, b % 2, 384:512], XT[s][:, b, :], ident[:, :])
                last.then_inc(s_xtr, 1)

            def transpose_p(k, s):
                pe.wait_ge(s_pn, k + 1)
                after(pe, s_pt, k)
                for b in range(4):
                    if b % 2 == 0:
                        pe.wait_ge(s_gev, k * 2 + (5 + b // 2) if runs(k + 2) else 2 * NSTEP)
                    for cc in range(2):
                        g = (b % 2) * 2 + cc
                        last = nc.tensor.transpose(psT[:, b // 2, g * P:(g + 1) * P],
                                                   Pn[s][:, b * 4 + 2 * cc:b * 4 + 2 * cc + 2, :].rearrange("p c u -> p (c u)"),
                                                   ident[:, :])
                    if b == 1:
                        last.then_inc(s_t0, 1)
                last.then_inc(s_t, 1)

            def context(k, s):
                pe.wait_ge(s_pt0, k + 1)
                pe.wait_ge(s_xb, k * 3 + (6 if runs(k + 1) else 3))
                after(pe, s_cev, k)
                for b in range(4):
                    if b == 2:
                        pe.wait_ge(s_pt, k + 1)
                    last = mm(psC[:, b // 2, (b % 2) * G4:(b % 2 + 1) * G4], XB[s][:, b, :], PT[:, b, :],
                              start=True, stop=True)
                last.then_inc(s_c, 1)

            def project(k):
                pe.wait_ge(s_cev, k + 1)
                after(pe, s_res, k)
                pe.wait_ge(s_sub, k * 2 + 5 if runs(k + 2) else 2 * NSTEP)
                pe.wait_ge(s_xb, k * 3 + 7 if runs(k + 2) else 3 * NSTEP)
                for b2 in range(2):
                    for g in range(4):
                        last = mm(psO[b2 * F:b2 * F + F, :], VOg[:, g, :], C[:, :, g, :].rearrange("p (r b) t -> p r b t", b=2)[:, :, b2, :],
                                  start=(g == 0), stop=(g == 3))
                last.then_inc(s_o, 1)

            def hidden(k, s, h):
                pe.wait_ge(s_xq[s], h * 96 + 96)
                after(pe, s_gelu, k * 2)
                for c in range(HCH):
                    for i, w in enumerate((w1_coarse, w1_fine)):
                        last = mm(psH[c], w[:, c * P:(c + 1) * P], xq[s][:, :], start=(i == 0), stop=(i == 1))
                last.then_inc(s_h, 1)

            def step(k, s, q=None, work=None):
                if isinstance(k, int) and k == NSTEP - 1:
                    pe.wait_ge(s_wcoarse, 2)
                    pe.wait_ge(s_wfine, 2)
                    pe.wait_ge(s_sub, 2 * NSTEP)
                    pe.wait_ge(s_xb, 3 * NSTEP)
                    pe.wait_ge(s_wcp, NR * NQ)
                    hidden(0, 0, 0)
                if runs(k + 1):
                    scores(k + 1, 1 - s)
                if runs(k + 1):
                    transpose_x(k + 1, 1 - s)
                if runs(k + 2):
                    make_g(k + 2, s)
                if work in TWO_ROUNDS:
                    broadcast(q * NR + TWO_ROUNDS[work], q, TWO_ROUNDS[work])
                if ln_end(k, q, work) and work != "ln":
                    variance(ln_end(k, q, work)[0])
                if runs(k):
                    transpose_p(k, s)
                if runs(k - 1) and not (isinstance(k, int) and k == NSTEP):
                    project(k - 1)
                if runs(k):
                    context(k, s)
                if work in ("ln", "ln begin", "ln2"):
                    mean(q + NQ if work == "ln2" else q, q, second=(work == "ln2"))
                if work == "ln":
                    variance(q)
                if work in TWO_ROUNDS:
                    broadcast(q * NR + (TWO_ROUNDS[work] + 1), q, TWO_ROUNDS[work] + 1)
                if work in ONE_ROUND:
                    broadcast(q * NR + ONE_ROUND[work], q, ONE_ROUND[work])

            pe.wait_ge(s_wsc, 1)
            for _ in range(WARM):
                mm(psC[:, 0, 0:T], prod[:, 0, 0, 0:P], prod[:, 0, 0, :], start=True, stop=True).then_inc(s_warm, 1)
            pe.wait_ge(s_wsc, 6)
            score(0, 0, QP)
            score(1, 0, QP)
            pe.wait_ge(s_sel, 3)
            for r in range(NR):
                broadcast(r, 0, r)
                score(2, 2 * r, 2 * r + 2)
            pe.wait_ge(s_aload, ALOADS)
            for h in range(H):
                last = mm(psMM[:, h * F:(h + 1) * F], k_sb[:, h, :, :].rearrange("r b d -> r (b d)"), q_sb[:, h, :], start=True, stop=True)
            last.then_inc(s_mm, 1)
            pe.wait_ge(s_zero, 1)
            mean(0, 0)
            score(3, 0, 2)
            variance(0)
            score(3, 2, QP)
            broadcast(NR, 1, 0)
            broadcast(NR + 1, 1, 1)
            pe.wait_ge(s_mmc, 2)
            pe.wait_ge(s_wsub, 2)
            pe.wait_ge(s_idt, 1)
            def gates(k, s):
                pe.wait_ge(s_gelu, k * 2 + 2)
                after(pe, s_fin, k - 1)
                for j, t0 in enumerate(STARTS):
                    for c in range(HCH):
                        mm(psL[s][:, j * E:(j + 1) * E], Hs[s][:, c, t0:t0 + P], wg_sb[:, c, :],
                           start=(c == 0), stop=(c == HCH - 1))
                for j, t0 in enumerate(STARTS):
                    last = nc.tensor.transpose(psR[s][:, j * F:(j + 1) * F], hq[s][:, t0:t0 + P], ident[0:F, 0:F])
                last.then_inc(s_lg, 1)

            def experts(k, s):
                pe.wait_ge(s_hf, k + 1)
                for j, t0 in enumerate(STARTS):
                    after(pe, s_z, k * 3 + (j - 2))
                    for c in range(HCH):
                        for i, (h, w) in enumerate(((h_coarse, wd_coarse), (h_coarse, wd_fine), (h_fine, wd_coarse))):
                            mm(psY[j], h[s][:, c, t0:t0 + P], w[:, c, :], start=(c == 0 and i == 0), stop=False)
                    mm(psY[j], ones3[:, :], bd3[:, :], start=False, stop=True).then_inc(s_y, 1)

            def fstep(k, s, h):
                gates(k, s)
                if runs(k + 1, NF):
                    hidden(k + 1, 1 - s, h + s)
                experts(k, s)

            attention_steps(pe, step)
            pe.wait_ge(s_pt, NSTEP)
            gates(0, 0)
            project(NSTEP - 1)
            hidden(1, 1, 0)
            mean(2 * NQ - 1, NQ - 1, second=True)
            pe.wait_ge(s_cev, NSTEP)
            pe.wait_ge(s_res, NSTEP)
            pe.wait_ge(s_bd, 5)
            experts(0, 0)
            variance(2 * NQ - 1)
            steps(pe, 1, NF - 1, 1, NF - 2, fstep)


_INS = ['x','L0_tok_w','L0_tok_b','L0_attn_Q','L0_attn_K','L0_attn_VO','L0_ffn_W1','L0_ffn_b1','L0_ffn_Wg','L0_ffn_bg','L0_ffn_Wd','L0_ffn_bd']
_OUTS = [((64, 47, 64), 'float32')]


def kernel(**inputs):
    import numpy as _np
    import concourse.bacc as _bacc
    from concourse import mybir as _mybir
    from concourse.bass_utils import run_bass_kernel_spmd as _run

    nc = _bacc.Bacc("TRN2", target_bir_lowering=False, num_devices=1)
    arrays, args = {}, []
    for name in _INS:
        a = _np.ascontiguousarray(inputs[name])
        arrays[f"in_{name}_dram"] = a
        args.append(nc.dram_tensor(f"in_{name}_dram", a.shape, _mybir.dt.from_np(a.dtype), kind="ExternalInput").ap())
    for i, (shape, dtype) in enumerate(_OUTS):
        dt = _mybir.dt.from_np(_np.dtype(dtype))
        args.append(nc.dram_tensor(f"out_{i}_dram", shape, dt, kind="ExternalOutput").ap())
    audio_tower_kernel(nc, *args)
    r = _run(nc, [arrays], core_ids=[0])
    got = tuple(r.results[0][f"out_{i}_dram"] for i in range(len(_OUTS)))
    return got[0]
```
